# Optimizing a Trainium2 kernel written in Bass

```python
import numpy as np
import jax
import jax.numpy as jnp

def _softmax(x, axis=-1):
    return jax.nn.softmax(x, axis=axis)

def _gelu(x):
    return jax.nn.gelu(x, approximate=True)

def _silu(x):
    return jax.nn.silu(x)

def _sigmoid(x):
    return jax.nn.sigmoid(x)

def _layernorm(x, axis=-1, eps=1e-05):
    m = jnp.mean(x, axis=axis, keepdims=True)
    v = jnp.var(x, axis=axis, keepdims=True)
    return (x - m) / jnp.sqrt(v + eps)

def _scatter_add(tgt, idx, src, axis=0):
    return tgt.at[idx].add(src)

def _segment_sum(src, seg, n):
    return jax.ops.segment_sum(src, seg, n)
kernel_name = 'mk_vit_tower_d1_tok_img1024_r4_1ed54f'

def setup_inputs(seed: int=0):
    np.random.seed(seed)
    _w = jnp.asarray

    def _rec_inputs():
        import jax
        import jax.numpy as jnp
        _rk = jax.random.key(seed)
        x = -0.000348323 + 0.999952 * jax.random.normal(jax.random.fold_in(_rk, 1), (64, 3, 224, 224), jnp.float32)
        return x
    x = _rec_inputs()

    def _L0_tok_setup():
        import jax, jax.numpy as jnp
        import numpy as np
        from jax import lax
        PATCH = 16
        key = jax.random.key(seed)
        k1, k2 = jax.random.split(key)
        B, C, IMG, HID = (32, 3, 96, 256)
        inputs = jax.random.normal(k1, (B, C, IMG, IMG), dtype=jnp.float32)
        flat = C * PATCH * PATCH
        W = jax.random.normal(k2, (flat, HID), dtype=jnp.float32) / np.sqrt(flat)
        return {'inputs': inputs, 'W': W}
    _L0_tok_all = _L0_tok_setup()
    _L0_tok_in = {k: v for k, v in _L0_tok_all.items() if k in ('W',)}
    del _L0_tok_all

    def _L0_attn_setup():
        import jax, jax.numpy as jnp
        import numpy as np
        DIM = 256
        KSIZE = 64
        HID = 1024
        B, L = (4, 1024)
        key = jax.random.key(seed)
        ks = jax.random.split(key, 10)
        s = lambda fan_in: 1.0 / np.sqrt(fan_in)
        return {'x': jax.random.normal(ks[0], (B, L, DIM), dtype=jnp.float32), 'in_w': jax.random.uniform(ks[1], (DIM, DIM), jnp.float32, -s(DIM), s(DIM)), 'in_b': jax.random.uniform(ks[2], (DIM,), jnp.float32, -s(DIM), s(DIM)), 'mod_w1': jax.random.uniform(ks[3], (DIM, HID), jnp.float32, -s(DIM), s(DIM)), 'mod_b1': jax.random.uniform(ks[4], (HID,), jnp.float32, -s(DIM), s(DIM)), 'mod_w2': jax.random.uniform(ks[5], (HID, DIM), jnp.float32, -s(HID), s(HID)), 'mod_b2': jax.random.uniform(ks[6], (DIM,), jnp.float32, -s(HID), s(HID)), 'kernel': jax.random.normal(ks[7], (DIM, KSIZE), dtype=jnp.float32), 'out_w': jax.random.uniform(ks[8], (DIM, DIM), jnp.float32, -s(DIM), s(DIM)), 'out_b': jax.random.uniform(ks[9], (DIM,), jnp.float32, -s(DIM), s(DIM))}
    _L0_attn_all = _L0_attn_setup()
    _L0_attn_in = {k: v for k, v in _L0_attn_all.items() if k in ('in_w', 'in_b', 'mod_w1', 'mod_b1', 'mod_w2', 'mod_b2', 'kernel', 'out_w', 'out_b')}
    del _L0_attn_all

    def _L0_ffn_setup():
        import jax, jax.numpy as jnp
        import numpy as np
        B, S, D = (8, 1024, 256)
        E, R, K = (6, 16, 2)
        key = jax.random.key(seed)
        ks = jax.random.split(key, 9)
        sc = 0.02
        return {'x': jax.random.normal(ks[0], (B, S, D), jnp.float32), 'base_W': jax.random.normal(ks[1], (D, D), jnp.float32) * sc, 'base_b': jax.random.normal(ks[2], (D,), jnp.float32) * sc, 'shared_A': jax.random.normal(ks[3], (R, D), jnp.float32) * sc, 'shared_B': jax.random.normal(ks[4], (D, R), jnp.float32) * sc, 'routed_A': jax.random.normal(ks[5], (E, R, D), jnp.float32) * sc, 'routed_B': jax.random.normal(ks[6], (E, D, R), jnp.float32) * sc, 'router_W': jax.random.normal(ks[7], (E, D), jnp.float32) * sc, 'router_b': jax.random.normal(ks[8], (E,), jnp.float32) * sc}
    _L0_ffn_all = _L0_ffn_setup()
    _L0_ffn_in = {k: v for k, v in _L0_ffn_all.items() if k in ('base_W', 'base_b', 'shared_A', 'shared_B', 'routed_A', 'routed_B', 'router_W', 'router_b')}
    del _L0_ffn_all
    return {'x': x, 'L0_tok_W': _L0_tok_in['W'], 'L0_attn_in_w': _L0_attn_in['in_w'], 'L0_attn_in_b': _L0_attn_in['in_b'], 'L0_attn_mod_w1': _L0_attn_in['mod_w1'], 'L0_attn_mod_b1': _L0_attn_in['mod_b1'], 'L0_attn_mod_w2': _L0_attn_in['mod_w2'], 'L0_attn_mod_b2': _L0_attn_in['mod_b2'], 'L0_attn_kernel': _L0_attn_in['kernel'], 'L0_attn_out_w': _L0_attn_in['out_w'], 'L0_attn_out_b': _L0_attn_in['out_b'], 'L0_ffn_base_W': _L0_ffn_in['base_W'], 'L0_ffn_base_b': _L0_ffn_in['base_b'], 'L0_ffn_shared_A': _L0_ffn_in['shared_A'], 'L0_ffn_shared_B': _L0_ffn_in['shared_B'], 'L0_ffn_routed_A': _L0_ffn_in['routed_A'], 'L0_ffn_routed_B': _L0_ffn_in['routed_B'], 'L0_ffn_router_W': _L0_ffn_in['router_W'], 'L0_ffn_router_b': _L0_ffn_in['router_b']}

def reference(x, L0_tok_W, L0_attn_in_w, L0_attn_in_b, L0_attn_mod_w1, L0_attn_mod_b1, L0_attn_mod_w2, L0_attn_mod_b2, L0_attn_kernel, L0_attn_out_w, L0_attn_out_b, L0_ffn_base_W, L0_ffn_base_b, L0_ffn_shared_A, L0_ffn_shared_B, L0_ffn_routed_A, L0_ffn_routed_B, L0_ffn_router_W, L0_ffn_router_b):
    import jax
    import jax.numpy as jnp

    def _L0_tok_ref(inputs, W):
        import jax, jax.numpy as jnp
        import numpy as np
        from jax import lax
        PATCH = 16
        B, C, H, Wimg = inputs.shape
        patches = lax.conv_general_dilated_patches(inputs, filter_shape=[PATCH, PATCH], window_strides=[PATCH, PATCH], padding='VALID', dimension_numbers=('NCHW', 'HWIO', 'NCHW'))
        patches = patches.reshape(B, -1, C * PATCH * PATCH)
        return jnp.einsum('bnf,fh->bnh', patches, W)

    def _L0_attn_ref(x, in_w, in_b, mod_w1, mod_b1, mod_w2, mod_b2, kernel, out_w, out_b):
        import jax, jax.numpy as jnp
        import numpy as np
        DIM = 256
        KSIZE = 64
        HID = 1024
        B, L = (4, 1024)
        Lx = x.shape[1]
        x_proj = x @ in_w + in_b
        h = jax.nn.gelu(x @ mod_w1 + mod_b1, approximate=False)
        mod = h @ mod_w2 + mod_b2
        modulated = x_proj * mod
        x_fft = jnp.fft.rfft(modulated.transpose(0, 2, 1), n=Lx)
        k_fft = jnp.fft.rfft(kernel, n=Lx)
        y = jnp.fft.irfft(x_fft * k_fft[None], n=Lx).transpose(0, 2, 1)
        return y @ out_w + out_b

    def _L0_ffn_ref(x, base_W, base_b, shared_A, shared_B, routed_A, routed_B, router_W, router_b):
        import jax, jax.numpy as jnp
        import numpy as np
        B, S, D = (8, 1024, 256)
        E, R, K = (6, 16, 2)
        base_out = jax.lax.stop_gradient(jnp.einsum('bsi,oi->bso', x, base_W) + base_b)
        shared_out = jnp.einsum('bsr,or->bso', jnp.einsum('bsi,ri->bsr', x, shared_A), shared_B)
        logits = jnp.einsum('bsi,ei->bse', x, router_W) + router_b
        gate = jax.nn.softmax(logits, axis=-1)
        topk_w, topk_i = jax.lax.top_k(gate, K)
        sparse_w = jnp.sum(jax.nn.one_hot(topk_i, E, dtype=gate.dtype) * topk_w[..., None], axis=-2)
        sparse_w = sparse_w / (jnp.sum(sparse_w, axis=-1, keepdims=True) + 1e-06)
        h = jnp.einsum('bsi,eri->bser', x, routed_A)
        routed_outs = jnp.einsum('bser,eor->bseo', h, routed_B)
        routed_out = jnp.einsum('bseo,bse->bso', routed_outs, sparse_w)
        return base_out + shared_out + routed_out
    h = _L0_tok_ref(x, L0_tok_W)
    h = h + _L0_attn_ref(_layernorm(h, axis=-1), L0_attn_in_w, L0_attn_in_b, L0_attn_mod_w1, L0_attn_mod_b1, L0_attn_mod_w2, L0_attn_mod_b2, L0_attn_kernel, L0_attn_out_w, L0_attn_out_b)
    h = h + _L0_ffn_ref(_layernorm(h, axis=-1), L0_ffn_base_W, L0_ffn_base_b, L0_ffn_shared_A, L0_ffn_shared_B, L0_ffn_routed_A, L0_ffn_routed_B, L0_ffn_router_W, L0_ffn_router_b)
    return h

_drawn_inputs = setup_inputs


def setup_inputs(seed=0):
    import zlib

    import numpy as np

    out = dict(_drawn_inputs(seed))
    spreads = {}
    factors = {'L0_ffn_base_b': 3.289,
     'L0_ffn_routed_A': 3.711,
     'L0_ffn_routed_B': 3.706,
     'L0_ffn_router_W': 4.55,
     'L0_ffn_router_b': 8.0,
     'L0_ffn_shared_A': 2.715,
     'L0_ffn_shared_B': 2.72}
    for name, (base, spread) in spreads.items():
        noise = np.random.default_rng([zlib.crc32(name.encode()), seed]).standard_normal(out[name].shape)
        drawn = base * np.exp(spread * noise) if base else spread * noise
        out[name] = jnp.asarray(drawn.astype(out[name].dtype))
    for name, factor in factors.items():
        out[name] = (out[name] * factor).astype(out[name].dtype)
    return out
```

```python
from contextlib import ExitStack

import numpy as np

import concourse.bass as bass
from concourse import mybir

F32 = mybir.dt.float32
F32R = mybir.dt.float32r
I32 = mybir.dt.int32
ACT = mybir.ActivationFunctionType
ALU = mybir.AluOpType
AX_X = mybir.AxisListType.X

P = 128
IMAGES, CHANNELS, SIDE, PATCH = 64, 3, 224, 16
GRID = SIDE // PATCH
N_TOK = GRID * GRID
FLAT = CHANNELS * PATCH * PATCH
DIM = 256
HID = 1024
TAPS = 64
EXPERTS, RANK = 6, 16
ROUTED = EXPERTS * RANK
ROUTE_COLS = ROUTED + EXPERTS
LN_EPS = 1e-5
GATE_EPS = 1e-6

PAIR = 2
GROUPS = IMAGES // PAIR
GT = PAIR * N_TOK
TILES = 4
TT = GT // TILES
KT = FLAT // P
DH = DIM // P
HC = HID // P
HALF = N_TOK // 2
NF = HALF + 1
BANK = 512
CONSTS = 10
RSQRT_MAGIC = 1597463007.0
NEWTON = 3
TINY = 1.1754944e-38

LN_STEPS = 6 + 2 + 3 * NEWTON + 1
GATE_STEPS = 13


def exists(g):
    return 0 <= g < GROUPS if isinstance(g, int) else True


def tower_program(nc: bass.Bass, xg, tok_w, in_w, w1, w2, taps_t, out_w, base_wt,
                  shared_a, shared_bt, route_w, routed_bt, biases_d, ident_d, cos_fwd_d, sin_fwd_d, cos_inv_d,
                  sin_inv_d, cos_tap_d, sin_tap_d, rank_thr_d, out):
    ctx = ExitStack()
    with ctx:
        def sb(name, shape, dt=F32):
            return ctx.enter_context(nc.sbuf_tensor(name, shape, dt))

        def sem(name):
            return ctx.enter_context(nc.semaphore(name))

        def pair(name, shape):
            return sb(name + "_h", shape, F32R), sb(name + "_l", shape, F32R)

        tokw_h, tokw_l = pair("tokw", [P, KT, DIM])
        inw_h, inw_l = pair("inw", [P, DH, DIM])
        w1_h, w1_l = pair("w1", [P, DH, HID])
        w2_h, w2_l = pair("w2", [P, HC, DIM])
        outw_h, outw_l = pair("outw", [P, DH, DIM])
        route_h, route_l = pair("route", [P, DH, ROUTE_COLS])
        base_h, base_l = pair("base", [P, DH, DIM])
        routedb_h, routedb_l = pair("routedb", [ROUTED, DIM])
        dft_h, dft_l = pair("dft", [NF, 2, 100])
        cos_inv = sb("cos_inv", [NF, N_TOK])
        sin_inv = sb("sin_inv", [NF, N_TOK])
        spec_k = sb("spec_k", [NF, 2, PAIR * DIM])
        ident = sb("ident", [P, P])
        rank_thr = sb("rank_thr", [TT, TILES * EXPERTS * EXPERTS])
        biases = sb("biases", [P, 4 * DH + HC + 1])
        in_bias = biases[:, 0:DH]
        b2_bias = biases[:, DH:2 * DH]
        out_bias = biases[:, 2 * DH:3 * DH]
        base_bias = biases[:, 3 * DH:4 * DH]
        b1_bias = biases[:, 4 * DH:4 * DH + HC]
        route_bias = biases[0:ROUTE_COLS, 4 * DH + HC:4 * DH + HC + 1]

        patches = sb("patches", [P, KT, GT])
        patches_h, patches_l = pair("patches", [P, KT, GT])
        h_sb = sb("h_sb", [P, 2, DH, GT])
        norm1 = sb("norm1", [TT, TILES, DIM])
        norm2 = sb("norm2", [TT, TILES, DIM])
        x1_h, x1_l = pair("x1", [P, DH, GT])
        x2_h, x2_l = pair("x2", [P, DH, GT])
        x_proj = sb("x_proj", [P, DH, GT])
        gelu = sb("gelu", [P, 4, GT])
        gelu_h, gelu_l = pair("gelu", [P, HC, GT])
        modulated = sb("modulated", [P, DH, PAIR, N_TOK])
        folded = sb("folded", [P, DH, 2, PAIR, NF])
        fold_h, fold_l = pair("fold", [NF, 2, PAIR * DIM])
        prod = sb("prod", [P, 2, 2, PAIR * DIM])
        spec_y = sb("spec_y", [NF, 2, PAIR * DIM])
        y_h, y_l = pair("y", [P, DH, GT])
        h2_sb = sb("h2_sb", [P, DH, GT])
        route_sb = sb("route_sb", [ROUTE_COLS, GT])
        gated = sb("gated", [TT, TILES, ROUTED])
        gated_h, gated_l = pair("gated", [ROUTED, GT])
        result = sb("result", [P, DH, GT])
        stage = prod[:, :, :, :].rearrange("p a b n -> p (a b n)")
        taps = sb("taps", [TAPS, DIM])
        tap_mats = sb("tap_mats", [TAPS, 2, 100])
        shared_sb = sb("shared_sb", [RANK, 2 * DIM])
        bn = sb("bn", [TT, 2, TILES, 6])
        mean_var = sb("mean_var", [TT, 2, TILES, 2])
        ln_tmp = sb("ln_tmp", [TT, 2, 10 + 3 * NEWTON, TILES])
        gate_small = sb("gate_small", [TT, 8, TILES])
        gate_wide = sb("gate_wide", [TT, 6, TILES, EXPERTS])
        gate_cmp = sb("gate_cmp", [TT, 2, TILES, EXPERTS, EXPERTS])

        big = [ctx.enter_context(nc.psum_tensor(f"big{n}", [P, BANK], F32)) for n in range(3)]
        turn = ctx.enter_context(nc.psum_tensor("turn", [P, 2, BANK], F32))
        turn2 = ctx.enter_context(nc.psum_tensor("turn2", [P, 2, BANK], F32))
        gate_ps = ctx.enter_context(nc.psum_tensor("gate_ps", [P, BANK], F32))

        weight_in = [sem(f"weight_in{n}") for n in range(9)]
        const_in = sem("const_in")
        patches_in = sem("patches_in")
        result_out = sem("result_out")
        pad_zero = sem("pad_zero")
        weight_hi = sem("weight_hi")
        weight_lo = sem("weight_lo")
        setup_mm = sem("setup_mm")
        spectrum_ready = sem("spectrum_ready")
        base_sum = sem("base_sum")
        pe_embed = sem("pe_embed")
        pe_turn_h = sem("pe_turn_h")
        pe_turn_x1 = sem("pe_turn_x1")
        pe_in = sem("pe_in")
        pe_w1 = sem("pe_w1")
        pe_w2 = sem("pe_w2")
        pe_turn_fold = sem("pe_turn_fold")
        pe_dft = sem("pe_dft")
        pe_idft = sem("pe_idft")
        pe_out = sem("pe_out")
        pe_turn_h2 = sem("pe_turn_h2")
        pe_turn_x2 = sem("pe_turn_x2")
        pe_route = sem("pe_route")
        pe_turn_route = sem("pe_turn_route")
        pe_turn_gated = sem("pe_turn_gated")
        pe_ffn = sem("pe_ffn")
        act_patches_hi = sem("act_patches_hi")
        act_h = sem("act_h")
        act_norm1 = sem("act_norm1")
        act_x1_hi = sem("act_x1_hi")
        act_in = sem("act_in")
        act_gelu = sem("act_gelu")
        act_gelu_hi = sem("act_gelu_hi")
        act_fold_hi = sem("act_fold_hi")
        act_y_hi = sem("act_y_hi")
        act_norm2 = sem("act_norm2")
        act_x2_hi = sem("act_x2_hi")
        act_route = sem("act_route")
        act_exp = sem("act_exp")
        act_gated_hi = sem("act_gated_hi")
        dve_ln1 = sem("dve_ln1")
        dve_ln2 = sem("dve_ln2")
        dve_x1_lo = sem("dve_x1_lo")
        dve_gelu_lo = sem("dve_gelu_lo")
        dve_mod = sem("dve_mod")
        dve_fold_lo = sem("dve_fold_lo")
        dve_spec = sem("dve_spec")
        dve_y_lo = sem("dve_y_lo")
        dve_h2 = sem("dve_h2")
        dve_x2_lo = sem("dve_x2_lo")
        dve_gate = sem("dve_gate")
        gate_done = sem("gate_done")
        dve_gated_lo = sem("dve_gated_lo")
        dve_result = sem("dve_result")
        pool_patches_lo = sem("pool_patches_lo")
        pool_fold = sem("pool_fold")

        out_v = out.rearrange("(m p) t -> p m t", p=P)

        gh = gelu[:, :, :].rearrange("p k t -> p (k t)")
        splits = [
            (tok_w.rearrange("(k p) n -> p k n", p=P), stage[:, 0:KT * DIM], tokw_h, tokw_l),
            (in_w.rearrange("(k p) n -> p k n", p=P), gh[:, 0:DH * DIM], inw_h, inw_l),
            (out_w.rearrange("(k p) n -> p k n", p=P), gh[:, DH * DIM:2 * DH * DIM], outw_h, outw_l),
            (route_w.rearrange("(k p) n -> p k n", p=P), gh[:, 2 * DH * DIM:2 * DH * DIM + DH * ROUTE_COLS],
             route_h, route_l),
            (routed_bt, norm2[0:ROUTED, 0, :], routedb_h, routedb_l),
            (w1.rearrange("(k p) n -> p k n", p=P), stage, w1_h, w1_l),
            (w2.rearrange("(k p) n -> p k n", p=P), stage, w2_h, w2_l),
        ]

        block = ctx.enter_context(nc.Block())

        @block.sync
        def _(sp):
            def const(dst, src):
                sp.dma_start(dst, src).then_inc(const_in, 16)

            sp.dma_start(stage[:, 0:KT * DIM].rearrange("p (k n) -> p k n", k=KT), splits[0][0])\
                .then_inc(weight_in[0], 16)
            sp.dma_start(patches[:, :, :], xg[0]).then_inc(patches_in, 16)
            const(ident[:, :], ident_d)
            for n in range(1, 5):
                src, dst = splits[n][0], splits[n][1]
                if n < 4:
                    dst = dst.rearrange("p (k n) -> p k n", k=DH)
                sp.dma_start(dst, src).then_inc(weight_in[n], 16)
            sp.dma_start(spec_y[:, 0, 0:NF], cos_fwd_d).then_inc(weight_in[7], 16)
            sp.dma_start(spec_y[:, 1, 0:NF], sin_fwd_d).then_inc(weight_in[7], 16)
            sp.dma_start(x_proj[:, :, 0:DIM], base_wt.rearrange("(k p) n -> p k n", p=P)).then_inc(weight_in[8], 16)
            const(biases[:, :], biases_d)
            const(taps[:, :], taps_t)
            const(tap_mats[:, 0, 0:NF], cos_tap_d)
            const(tap_mats[:, 1, 0:NF], sin_tap_d)
            const(cos_inv[:, :], cos_inv_d)
            const(sin_inv[:, :], sin_inv_d)
            const(shared_sb[:, 0:DIM], shared_a)
            const(shared_sb[:, DIM:2 * DIM], shared_bt)
            const(rank_thr[:, :], rank_thr_d)
            for n, k in ((5, DH), (6, HC)):
                sp.wait_ge(weight_lo, 1 if n == 5 else 7)
                sp.dma_start(stage.rearrange("p (k n) -> p k n", k=k), splits[n][0])\
                    .then_inc(weight_in[n], 16)

            def step(i):
                front, tail = i, i - 3
                if exists(tail):
                    sp.wait_ge(dve_result, 2 * tail + 2)
                    sp.dma_start(out_v[:, :, bass.ds(tail * GT, GT)], result[:, :, :]).then_inc(result_out, 16)
                if exists(front) and (not isinstance(front, int) or front + 1 < GROUPS):
                    sp.wait_ge(pool_patches_lo, KT * front + KT)
                    sp.dma_start(patches[:, :, :], xg[bass.ds(front + 1, 1)].rearrange("g p k t -> p (g k) t"))\
                        .then_inc(patches_in, 16)

            for i in range(4):
                step(i)
            with sp.Fori(4, GROUPS - 2, 2) as i:
                step(i)
                step(i + 1)
            for i in range(GROUPS - 2, GROUPS + 3):
                step(i)
            sp.wait_ge(result_out, 16 * GROUPS)

        @block.gpsimd
        def _(pool):
            pool.memset(folded[:, :, :, :, :], 0.0).then_inc(pad_zero, 1)

            def patches_lo(g):
                for k in range(KT):
                    pool.wait_ge(act_patches_hi, KT * g + k + 1)
                    pool.tensor_tensor(patches_l[:, k, :], patches[:, k, :], patches_h[:, k, :].bitcast(F32),
                                       ALU.subtract).then_inc(pool_patches_lo, 1)

            def fold(g):
                for m in range(DH):
                    pool.wait_ge(dve_mod, DH * g + m + 1)
                    if m == 0:
                        if exists(g - 1):
                            pool.wait_ge(pe_turn_fold, g)
                        else:
                            pool.wait_ge(pad_zero, 1)
                    fwd = modulated[:, m, :, 1:NF]
                    back = modulated[:, m, :, N_TOK - 1:N_TOK - NF:-1]
                    pool.tensor_tensor(folded[:, m, 0, :, 1:NF], fwd, back, ALU.add)
                    pool.tensor_copy(folded[:, m, 0, :, 0:1], modulated[:, m, :, 0:1])
                    pool.tensor_tensor(folded[:, m, 1, :, 1:NF], fwd, back, ALU.subtract).then_inc(pool_fold, 1)

            def step(i):
                front, mid = i, i - 1
                if exists(front):
                    patches_lo(front)
                if exists(mid):
                    fold(mid)

            for i in range(4):
                step(i)
            with pool.Fori(4, GROUPS - 2, 2) as i:
                step(i)
                step(i + 1)
            for i in range(GROUPS - 2, GROUPS + 3):
                step(i)

        @block.scalar
        def _(act):
            def weight_split(n):
                src, stage_ap, hi, lo = splits[n]
                act.wait_ge(weight_in[n], 16)
                flat = hi[:, :] if len(hi.shape) == 2 else hi[:, :, :].rearrange("p k n -> p (k n)")
                act.activation(flat, stage_ap, ACT.Copy).then_inc(weight_hi, 1)

            def patches_hi(g, ks):
                for k in ks:
                    if k == 0:
                        act.wait_ge(patches_in, 16 * (g + 1))
                        if exists(g - 1):
                            act.wait_ge(pe_embed, DH * g)
                    act.activation(patches_h[:, k, :], patches[:, k, :], ACT.Copy).then_inc(act_patches_hi, 1)

            weight_split(0)
            patches_hi(0, range(KT))
            act.wait_ge(weight_in[7], 32)
            act.activation(dft_h[:, :, 0:NF], spec_y[:, :, 0:NF], ACT.Copy).then_inc(weight_hi, 1)
            for n in (1, 2, 3, 4, 5, 6):
                weight_split(n)
            act.wait_ge(base_sum, DH)
            act.activation(base_h[:, :, :], x_proj[:, :, 0:DIM], ACT.Copy).then_inc(weight_hi, 1)
            act.wait_ge(const_in, 16 * CONSTS)

            def step(i, par):
                front, mid, back, tail = i, i - 1, i - 2, i - 3
                if exists(mid):
                    for m in range(DH):
                        act.wait_ge(pe_in, DH * mid + m + 1)
                        if m == 0:
                            if exists(mid - 1):
                                act.wait_ge(dve_mod, DH * mid)
                            else:
                                act.wait_ge(weight_lo, 9)
                        act.activation(x_proj[:, m, :], big[m][:, 0:GT], ACT.Identity,
                                       bias=in_bias[:, m:m + 1]).then_inc(act_in, 1)
                if exists(tail):
                    act.wait_ge(dve_gate, GATE_STEPS * tail + 2)
                    act.activation(gate_wide[:, 1], gate_wide[:, 0], ACT.Exp).then_inc(act_exp, 1)

                def gelu_tile(k):
                    act.wait_ge(pe_w1, HC * mid + k + 1)
                    if k % 2 == 0:
                        if k >= 4:
                            act.wait_ge(dve_gelu_lo, 4 * mid + k // 2 - 1)
                        elif exists(mid - 1):
                            act.wait_ge(dve_gelu_lo, 4 * (mid - 1) + k // 2 + 3)
                    bank = (2, 0, 1, 2, 2, 0, 1, 2)[k]
                    act.activation(gelu[:, k % 4, :], big[bank][:, 0:GT], ACT.Gelu,
                                   bias=b1_bias[:, k:k + 1]).then_inc(act_gelu, 1)

                def gelu_hi(j):
                    act.wait_ge(act_gelu, HC * mid + 2 * j + 2)
                    s = (2 * j) % 4
                    act.activation(gelu_h[:, 2 * j:2 * j + 2, :], gelu[:, s:s + 2, :], ACT.Copy)\
                        .then_inc(act_gelu_hi, 1)

                split_patches = exists(front) and not (isinstance(i, int) and i == 0)
                if exists(mid):
                    gelu_tile(0)
                    gelu_tile(1)
                    gelu_hi(0)
                if exists(tail):
                    act.wait_ge(pe_turn_gated, tail + 1)
                    act.activation(gated_h[:, :], gate_ps[0:ROUTED, 0:GT], ACT.Copy).then_inc(act_gated_hi, 1)
                if exists(back):
                    act.wait_ge(pe_turn_fold, back + 1)
                    act.activation(fold_h[:, :, :], turn[0:NF, :, :], ACT.Copy).then_inc(act_fold_hi, 1)
                if exists(mid):
                    gelu_tile(2)
                    gelu_tile(3)
                    gelu_hi(1)
                if split_patches:
                    patches_hi(front, (0, 1))
                if exists(mid):
                    gelu_tile(4)
                if split_patches:
                    patches_hi(front, (2,))
                if exists(mid):
                    gelu_tile(5)
                    gelu_hi(2)
                if split_patches:
                    patches_hi(front, (3,))
                if exists(mid):
                    gelu_tile(6)
                if split_patches:
                    patches_hi(front, (4,))
                if exists(mid):
                    gelu_tile(7)
                    gelu_hi(3)
                if split_patches:
                    patches_hi(front, (5,))
                if exists(back):
                    act.wait_ge(pe_idft, back + 1)
                    act.activation(y_h[:, :, :], turn[:, :, 0:GT], ACT.Copy).then_inc(act_y_hi, 1)
                if exists(front):
                    for m in range(DH):
                        act.wait_ge(pe_embed, DH * front + m + 1)
                        if exists(front - 2):
                            act.wait_ge(dve_h2, DH * (front - 2) + m + 1)
                        act.activation(h_sb[:, par, m, :], big[0][:, 0:GT], ACT.Copy).then_inc(act_h, 1)
                if exists(back):
                    act.wait_ge(dve_ln2, LN_STEPS * back + LN_STEPS)
                    for t in range(TILES):
                        ins = act.activation(norm2[:, t, :], turn2[0:TT, t // 2, DIM * (t % 2):DIM * (t % 2) + DIM],
                                             ACT.Identity, bias=ln_tmp[:, 1, 1, t:t + 1],
                                             scale=ln_tmp[:, 1, 0, t:t + 1])
                    ins.then_inc(act_norm2, 1)
                if exists(back):
                    act.wait_ge(pe_turn_x2, back + 1)
                    if exists(back - 1):
                        act.wait_ge(pe_ffn, DH * back)
                    act.activation(x2_h[:, :, :], turn2[:, :, 0:GT], ACT.Copy).then_inc(act_x2_hi, 1)
                if exists(front):
                    act.wait_ge(dve_ln1, LN_STEPS * front + LN_STEPS)
                    for t in range(TILES):
                        ins = act.activation(norm1[:, t, :], turn[0:TT, t // 2, DIM * (t % 2):DIM * (t % 2) + DIM],
                                             ACT.Identity, bias=ln_tmp[:, 0, 1, t:t + 1],
                                             scale=ln_tmp[:, 0, 0, t:t + 1])
                    ins.then_inc(act_norm1, 1)
                if exists(front):
                    act.wait_ge(pe_turn_x1, front + 1)
                    act.activation(x1_h[:, :, :], turn[:, :, 0:GT], ACT.Copy).then_inc(act_x1_hi, 1)
                if exists(back):
                    act.wait_ge(pe_route, back + 1)
                    act.activation(route_sb[:, :], gate_ps[0:ROUTE_COLS, 0:GT], ACT.Identity,
                                   bias=route_bias).then_inc(act_route, 1)

            for i in range(4):
                step(i, i % 2)
            with act.Fori(4, GROUPS - 2, 2) as i:
                step(i, 0)
                step(i + 1, 1)
            for i in range(GROUPS - 2, GROUPS + 3):
                step(i, i % 2)

        @block.vector
        def _(dve):
            def weight_split(n, order):
                src, stage_ap, hi, lo = splits[n]
                dve.wait_ge(weight_hi, order)
                if len(hi.shape) == 2:
                    h, l = hi[:, :], lo[:, :]
                else:
                    h, l = (w[:, :, :].rearrange("p k n -> p (k n)") for w in (hi, lo))
                dve.tensor_tensor(l, stage_ap, h.bitcast(F32), ALU.subtract).then_inc(weight_lo, 1)

            weight_split(0, 1)
            dve.wait_ge(weight_hi, 2)
            dve.tensor_tensor(dft_l[:, :, 0:NF], spec_y[:, :, 0:NF], dft_h[:, :, 0:NF].bitcast(F32),
                              ALU.subtract).then_inc(weight_lo, 1)
            for order, n in enumerate((1, 2, 3, 4)):
                weight_split(n, order + 3)
            weight_split(5, 7)
            dve.wait_ge(setup_mm, 2 + DH)
            for img in range(PAIR):
                ins = dve.tensor_copy(spec_k[:, :, img * DIM:(img + 1) * DIM], turn2[0:NF, :, 0:DIM])
            ins.then_inc(spectrum_ready, 1)
            dve.wait_ge(weight_in[8], 16)
            for k in range(DH):
                dve.tensor_tensor(x_proj[:, k, 0:DIM], turn2[:, k, DIM:2 * DIM], x_proj[:, k, 0:DIM], ALU.add)\
                    .then_inc(base_sum, 1)
            weight_split(6, 8)
            dve.wait_ge(weight_hi, 9)
            dve.tensor_tensor(base_l[:, :, :], x_proj[:, :, 0:DIM], base_h[:, :, :].bitcast(F32), ALU.subtract)\
                .then_inc(weight_lo, 1)
            dve.wait_ge(const_in, 16 * CONSTS)

            def layer_norm(g, which, ps, ready, chain):
                done = [0]
                tmp = ln_tmp[:, which]

                def link(ins, wait=True):
                    done[0] += 1
                    ins.then_inc(chain, 1)
                    if wait and done[0] < LN_STEPS:
                        dve.wait_ge(chain, LN_STEPS * g + done[0])

                dve.wait_ge(ready, g + 1)
                for t in range(TILES):
                    ins = dve.bn_stats(bn[:, which, t, :], ps[0:TT, t // 2, DIM * (t % 2):DIM * (t % 2) + DIM])
                link(ins)
                mean_m2 = mean_var[:, which]
                link(dve.tensor_reduce(mean_m2, bn[:, which].rearrange("p t (x f) -> p t f x", x=2)[:, :, 1:3, :],
                                       AX_X, ALU.add), wait=False)
                diff, within, between = tmp[:, 3 * NEWTON + 7], tmp[:, 3 * NEWTON + 8], tmp[:, 3 * NEWTON + 9]
                link(dve.tensor_tensor(diff, bn[:, which, :, 1], bn[:, which, :, 4], ALU.subtract))
                link(dve.tensor_scalar(within, mean_m2[:, :, 1], 1.0 / DIM, LN_EPS, ALU.mult, ALU.add), wait=False)
                link(dve.scalar_tensor_tensor(out=between, in0=diff, scalar=0.25, in1=diff, op0=ALU.mult,
                                              op1=ALU.mult))
                v = tmp[:, 2]
                link(dve.tensor_tensor(v, within, between, ALU.add))
                link(dve.tensor_scalar(tmp[:, 3].bitcast(I32), v.bitcast(I32), 1, None, ALU.logical_shift_right))
                link(dve.tensor_scalar(tmp[:, 4].bitcast(I32), tmp[:, 3].bitcast(I32), -1.0, RSQRT_MAGIC,
                                       ALU.mult, ALU.add))
                r = tmp[:, 4]
                for n in range(NEWTON):
                    sq, half = tmp[:, 5 + 3 * n], tmp[:, 6 + 3 * n]
                    new = tmp[:, 7 + 3 * n] if n < NEWTON - 1 else tmp[:, 0]
                    link(dve.tensor_tensor(sq, r, r, ALU.mult))
                    link(dve.scalar_tensor_tensor(out=half, in0=sq, scalar=-0.5, in1=v, op0=ALU.mult, op1=ALU.mult))
                    link(dve.scalar_tensor_tensor(out=new, in0=half, scalar=1.5, in1=r, op0=ALU.add, op1=ALU.mult))
                    r = new
                link(dve.scalar_tensor_tensor(out=tmp[:, 1], in0=mean_m2[:, :, 0], scalar=-0.5, in1=r, op0=ALU.mult,
                                              op1=ALU.mult))
                assert done[0] == LN_STEPS

            def over_experts(a):
                return a.rearrange("p (t a) -> p t a", a=1).broadcast_to([TT, TILES, EXPERTS])

            def gate(g):
                done = [0]

                def link(ins, wait=True):
                    done[0] += 1
                    ins.then_inc(dve_gate, 1)
                    if wait:
                        dve.wait_ge(dve_gate, GATE_STEPS * g + done[0])

                rows = gate_ps[0:TT, 0:TILES * ROUTE_COLS].rearrange("p (t c) -> p t c", t=TILES)
                logits = rows[:, :, ROUTED:ROUTE_COLS]
                small = lambda n: gate_small[:, n, :]
                dve.wait_ge(pe_turn_route, g + 1)
                link(dve.tensor_reduce(small(0), logits, AX_X, ALU.max))
                link(dve.tensor_tensor(gate_wide[:, 0], logits, over_experts(small(0)), ALU.subtract), wait=False)
                dve.wait_ge(act_exp, g + 1)
                link(dve.tensor_reduce(small(1), gate_wide[:, 1], AX_X, ALU.add))
                link(dve.reciprocal(small(2), small(1)))
                gates = gate_wide[:, 2]
                link(dve.tensor_tensor(gates, gate_wide[:, 1], over_experts(small(2)), ALU.mult))
                e4 = [TT, TILES, EXPERTS, EXPERTS]
                other = gates.rearrange("p t (a e) -> p t a e", a=1).broadcast_to(e4)
                own = gates.rearrange("p t (e a) -> p t e a", a=1).broadcast_to(e4)
                link(dve.tensor_tensor(gate_cmp[:, 0], other, own, ALU.subtract))
                flat = lambda n: gate_cmp[:, n].rearrange("p t e f -> p (t e f)")
                link(dve.tensor_tensor(flat(1), flat(0), rank_thr[:, :], ALU.is_gt))
                link(dve.tensor_reduce(gate_wide[:, 3], gate_cmp[:, 1], AX_X, ALU.add))
                wide = lambda n: gate_wide[:, n].rearrange("p t e -> p (t e)")
                link(dve.scalar_tensor_tensor(out=wide(4), in0=wide(3), scalar=1.5, in1=wide(2), op0=ALU.is_lt,
                                              op1=ALU.mult))
                link(dve.tensor_reduce(small(3), gate_wide[:, 4], AX_X, ALU.add))
                link(dve.tensor_scalar(small(4), small(3), GATE_EPS, None, ALU.add))
                link(dve.reciprocal(small(5), small(4)))
                link(dve.tensor_tensor(gate_wide[:, 5], gate_wide[:, 4], over_experts(small(5)), ALU.mult))
                assert done[0] == GATE_STEPS
                hidden = rows[:, :, 0:ROUTED].rearrange("p t (e r) -> p t e r", r=RANK)
                weight = gate_wide[:, 5].rearrange("p t (e a) -> p t e a", a=1)\
                    .broadcast_to([TT, TILES, EXPERTS, RANK])
                dve.tensor_tensor(gated[:, :, :].rearrange("p t (e r) -> p t e r", r=RANK), hidden, weight,
                                  ALU.mult).then_inc(gate_done, 1)

            def gelu_lo(g, j):
                dve.wait_ge(act_gelu_hi, 4 * g + j + 1)
                s = (2 * j) % 4
                dve.tensor_tensor(gelu_l[:, 2 * j:2 * j + 2, :], gelu[:, s:s + 2, :],
                                  gelu_h[:, 2 * j:2 * j + 2, :].bitcast(F32), ALU.subtract).then_inc(dve_gelu_lo, 1)

            def step(i, par):
                front, mid, back, tail = i, i - 1, i - 2, i - 3
                if exists(tail):
                    gate(tail)
                if exists(mid):
                    gelu_lo(mid, 0)
                if exists(tail):
                    dve.wait_ge(act_gated_hi, tail + 1)
                    dve.tensor_tensor(gated_l[:, :], gate_ps[0:ROUTED, 0:GT], gated_h[:, :].bitcast(F32),
                                      ALU.subtract).then_inc(dve_gated_lo, 1)
                if exists(back):
                    dve.wait_ge(act_fold_hi, back + 1)
                    dve.tensor_tensor(fold_l[:, :, :], turn[0:NF, :, :], fold_h[:, :, :].bitcast(F32),
                                      ALU.subtract).then_inc(dve_fold_lo, 1)
                if exists(mid):
                    gelu_lo(mid, 1)
                if exists(tail):
                    for m in range(DH):
                        dve.wait_ge(pe_ffn, DH * tail + m + 1)
                        if m == 0 and exists(tail - 1):
                            dve.wait_ge(result_out, 16 * tail)
                        dve.scalar_tensor_tensor(out=result[:, m, :], in0=big[m][:, 0:GT],
                                                 scalar=base_bias[:, m:m + 1], in1=h2_sb[:, m, :], op0=ALU.add,
                                                 op1=ALU.add).then_inc(dve_result, 1)
                if exists(back):
                    dve.wait_ge(pe_dft, back + 1)
                    for c in range(2):
                        for x in range(2):
                            ins = dve.tensor_tensor(prod[0:NF, c, x, :], turn[0:NF, x, :], spec_k[:, c, :], ALU.mult)
                    ins.then_inc(dve_spec, 1)
                    dve.wait_ge(dve_spec, 3 * back + 1)
                    dve.tensor_tensor(spec_y[:, 0, :], prod[0:NF, 0, 0, :], prod[0:NF, 1, 1, :], ALU.subtract)\
                        .then_inc(dve_spec, 1)
                    dve.tensor_tensor(spec_y[:, 1, :], prod[0:NF, 0, 1, :], prod[0:NF, 1, 0, :], ALU.add)\
                        .then_inc(dve_spec, 1)
                if exists(mid):
                    gelu_lo(mid, 2)
                    gelu_lo(mid, 3)
                if exists(back):
                    dve.wait_ge(act_y_hi, back + 1)
                    dve.tensor_tensor(y_l[:, :, :], turn[:, :, 0:GT], y_h[:, :, :].bitcast(F32), ALU.subtract)\
                        .then_inc(dve_y_lo, 1)
                    for m in range(DH):
                        dve.wait_ge(pe_out, DH * back + m + 1)
                        dve.scalar_tensor_tensor(out=h2_sb[:, m, :], in0=big[1 + m][:, 0:GT],
                                                 scalar=out_bias[:, m:m + 1], in1=h_sb[:, par, m, :], op0=ALU.add,
                                                 op1=ALU.add).then_inc(dve_h2, 1)
                    layer_norm(back, 1, turn2, pe_turn_h2, dve_ln2)
                if exists(front):
                    layer_norm(front, 0, turn, pe_turn_h, dve_ln1)

                def modulate(m):
                    dve.wait_ge(pe_w2, DH * mid + m + 1)
                    dve.wait_ge(act_in, DH * mid + m + 1)
                    if exists(mid - 1):
                        dve.wait_ge(pool_fold, DH * (mid - 1) + m + 1)
                    dve.scalar_tensor_tensor(out=modulated[:, m, :, :].rearrange("p a t -> p (a t)"),
                                             in0=big[1 + m][:, 0:GT], scalar=b2_bias[:, m:m + 1],
                                             in1=x_proj[:, m, :], op0=ALU.add, op1=ALU.mult).then_inc(dve_mod, 1)

                if exists(mid):
                    modulate(0)
                if exists(back):
                    dve.wait_ge(act_x2_hi, back + 1)
                    dve.tensor_tensor(x2_l[:, :, :], turn2[:, :, 0:GT], x2_h[:, :, :].bitcast(F32), ALU.subtract)\
                        .then_inc(dve_x2_lo, 1)
                if exists(front):
                    dve.wait_ge(act_x1_hi, front + 1)
                    dve.tensor_tensor(x1_l[:, :, :], turn[:, :, 0:GT], x1_h[:, :, :].bitcast(F32), ALU.subtract)\
                        .then_inc(dve_x1_lo, 1)
                if exists(mid):
                    modulate(1)

            for i in range(4):
                step(i, i % 2)
            with dve.Fori(4, GROUPS - 2, 2) as i:
                step(i, 0)
                step(i + 1, 1)
            for i in range(GROUPS - 2, GROUPS + 3):
                step(i, i % 2)

        @block.tensor
        def _(pe):
            def mm3(ps, w_h, w_l, x_h, x_l, first, last):
                pe.matmul(ps, w_h, x_h, start=first, stop=False)
                pe.matmul(ps, w_h, x_l, start=False, stop=False)
                return pe.matmul(ps, w_l, x_h, start=False, stop=last)

            def embed(g, m):
                if m == 0:
                    if exists(g - 1):
                        pe.wait_ge(act_gelu, HC * (g - 1) + 6)
                    else:
                        pe.wait_ge(weight_lo, 1)
                else:
                    pe.wait_ge(act_h, DH * g + 1)
                for k in range(KT):
                    if m == 0:
                        pe.wait_ge(pool_patches_lo, KT * g + k + 1)
                    ins = mm3(big[0][:, 0:GT], tokw_h[:, k, m * P:(m + 1) * P], tokw_l[:, k, m * P:(m + 1) * P],
                              patches_h[:, k, :], patches_l[:, k, :], k == 0, k == KT - 1)
                ins.then_inc(pe_embed, 1)

            def to_tokens(ps, rows, signal):
                for t in range(TILES):
                    for m in range(DH):
                        c = DIM * (t % 2) + m * P
                        ins = pe.transpose(ps[0:TT, t // 2, c:c + P], rows[:, m, t * TT:(t + 1) * TT], ident[:, :])
                ins.then_inc(signal, 1)

            def to_features(ps, rows, signal):
                for m in range(DH):
                    for t in range(TILES):
                        ins = pe.transpose(ps[:, m, t * TT:(t + 1) * TT], rows[:, t, m * P:(m + 1) * P],
                                           ident[0:TT, 0:TT])
                ins.then_inc(signal, 1)

            def mlp_up(g, k, free, value):
                bank = (2, 0, 1, 2, 2, 0, 1, 2)[k]
                if free is not None:
                    pe.wait_ge(free, value)
                for c in range(DH):
                    ins = mm3(big[bank][:, 0:GT], w1_h[:, c, k * P:(k + 1) * P], w1_l[:, c, k * P:(k + 1) * P],
                              x1_h[:, c, :], x1_l[:, c, :], c == 0, c == DH - 1)
                ins.then_inc(pe_w1, 1)

            def mlp_down(g, m, cs):
                for c in cs:
                    if m == 0 and c % 2 == 0:
                        pe.wait_ge(dve_gelu_lo, 4 * g + c // 2 + 1)
                    ins = mm3(big[1 + m][:, 0:GT], w2_h[:, c, m * P:(m + 1) * P], w2_l[:, c, m * P:(m + 1) * P],
                              gelu_h[:, c, :], gelu_l[:, c, :], c == 0, c == HC - 1)
                if cs[-1] == HC - 1:
                    ins.then_inc(pe_w2, 1)

            pe.wait_ge(const_in, 16 * CONSTS)
            for c in range(2):
                pe.matmul(turn2[0:NF, c, 0:DIM], tap_mats[:, c, 0:NF], taps[:, :], start=True, stop=True)\
                    .then_inc(setup_mm, 1)
            for k in range(DH):
                pe.matmul(turn2[:, k, DIM:2 * DIM], shared_sb[:, k * P:(k + 1) * P], shared_sb[:, DIM:2 * DIM],
                          start=True, stop=True).then_inc(setup_mm, 1)

            def step(i, par):
                front, mid, back, tail = i, i - 1, i - 2, i - 3
                if exists(mid):
                    if not exists(mid - 1):
                        pe.wait_ge(weight_lo, 7)
                    pe.wait_ge(dve_x1_lo, mid + 1)
                    for m in range(DH):
                        if m == 1 and exists(back):
                            pe.wait_ge(dve_mod, DH * back + 1)
                        for c in range(DH):
                            ins = mm3(big[m][:, 0:GT], inw_h[:, c, m * P:(m + 1) * P],
                                      inw_l[:, c, m * P:(m + 1) * P], x1_h[:, c, :], x1_l[:, c, :],
                                      c == 0, c == DH - 1)
                        ins.then_inc(pe_in, 1)
                    if exists(back):
                        mlp_up(mid, 0, dve_mod, DH * back + 2)
                    else:
                        mlp_up(mid, 0, None, None)
                    mlp_up(mid, 1, act_in, DH * mid + 1)
                if exists(tail):
                    pe.wait_ge(gate_done, tail + 1)
                    for t in range(TILES):
                        ins = pe.transpose(gate_ps[0:ROUTED, t * TT:(t + 1) * TT], gated[:, t, :],
                                           ident[0:TT, 0:TT])
                    ins.then_inc(pe_turn_gated, 1)
                if exists(back):
                    pe.wait_ge(pool_fold, DH * back + 2)
                    for x in range(2):
                        for img in range(PAIR):
                            for m in range(DH):
                                c = img * DIM + m * P
                                ins = pe.transpose(turn[0:NF, x, c:c + P], folded[:, m, x, img, :], ident[:, :])
                    ins.then_inc(pe_turn_fold, 1)
                if exists(mid):
                    mlp_up(mid, 2, act_in, DH * mid + 2)
                    mlp_up(mid, 3, act_gelu, HC * mid + 1)
                if exists(tail):
                    for m in range(DH):
                        if exists(mid):
                            pe.wait_ge(act_gelu, HC * mid + 2 + m)
                        elif m == 0 and exists(tail - 1):
                            pe.wait_ge(dve_result, DH * (tail - 1) + 1)
                        for c in range(DH):
                            mm3(big[m][:, 0:GT], base_h[:, c, m * P:(m + 1) * P], base_l[:, c, m * P:(m + 1) * P],
                                x2_h[:, c, :], x2_l[:, c, :], c == 0, False)
                        if m == 0:
                            pe.wait_ge(dve_gated_lo, tail + 1)
                        mm3(big[m][:, 0:GT], routedb_h[:, m * P:(m + 1) * P], routedb_l[:, m * P:(m + 1) * P],
                            gated_h[:, :], gated_l[:, :], False, True).then_inc(pe_ffn, 1)
                if exists(back):
                    pe.wait_ge(dve_fold_lo, back + 1)
                    for x in range(2):
                        ins = mm3(turn[0:NF, x, :], dft_h[:, x, 0:NF], dft_l[:, x, 0:NF], fold_h[:, x, :],
                                  fold_l[:, x, :], True, True)
                    ins.then_inc(pe_dft, 1)
                if exists(mid):
                    mlp_up(mid, 4, act_gelu, HC * mid + 4)
                    for k in (5, 6):
                        if exists(tail):
                            mlp_up(mid, k, dve_result, DH * tail + k - 4)
                        else:
                            mlp_up(mid, k, act_gelu, HC * mid + k - 3)
                    mlp_up(mid, 7, act_gelu, HC * mid + 5)
                if exists(back):
                    if not exists(back - 1):
                        pe.wait_ge(const_in, 16 * CONSTS)
                    pe.wait_ge(dve_spec, 3 * back + 3)
                    for m in range(DH):
                        for img in range(PAIR):
                            c = img * DIM + m * P
                            ps = turn[:, m, img * N_TOK:(img + 1) * N_TOK]
                            pe.matmul(ps, spec_y[:, 0, c:c + P], cos_inv[:, :], start=True, stop=False)
                            ins = pe.matmul(ps, spec_y[:, 1, c:c + P], sin_inv[:, :], start=False, stop=True)
                    ins.then_inc(pe_idft, 1)
                if exists(front):
                    embed(front, 0)
                if exists(back):
                    pe.wait_ge(dve_y_lo, back + 1)
                    for m in range(DH):
                        if exists(mid):
                            pe.wait_ge(act_gelu, HC * mid + 7 + m)
                        elif m == 0 and exists(tail):
                            pe.wait_ge(dve_result, DH * tail + 2)
                        for c in range(DH):
                            ins = mm3(big[1 + m][:, 0:GT], outw_h[:, c, m * P:(m + 1) * P],
                                      outw_l[:, c, m * P:(m + 1) * P], y_h[:, c, :], y_l[:, c, :],
                                      c == 0, c == DH - 1)
                        ins.then_inc(pe_out, 1)
                if exists(front):
                    embed(front, 1)
                if exists(back):
                    pe.wait_ge(dve_h2, DH * back + 2)
                    to_tokens(turn2, h2_sb, pe_turn_h2)
                if exists(mid):
                    if not exists(mid - 1):
                        pe.wait_ge(weight_lo, 9)
                    mlp_down(mid, 0, range(4))
                if exists(front):
                    pe.wait_ge(act_h, DH * front + 2)
                    to_tokens(turn, h_sb[:, par], pe_turn_h)
                if exists(mid):
                    mlp_down(mid, 0, range(4, 8))
                if exists(back):
                    pe.wait_ge(act_norm2, back + 1)
                    to_features(turn2, norm2, pe_turn_x2)
                if exists(mid):
                    mlp_down(mid, 1, range(4))
                if exists(front):
                    pe.wait_ge(act_norm1, front + 1)
                    to_features(turn, norm1, pe_turn_x1)
                if exists(back):
                    pe.wait_ge(dve_x2_lo, back + 1)
                    for c in range(DH):
                        ins = mm3(gate_ps[0:ROUTE_COLS, 0:GT], route_h[:, c, :], route_l[:, c, :], x2_h[:, c, :],
                                  x2_l[:, c, :], c == 0, c == DH - 1)
                    ins.then_inc(pe_route, 1)
                if exists(mid):
                    mlp_down(mid, 1, range(4, 8))
                if exists(back):
                    pe.wait_ge(act_route, back + 1)
                    for t in range(TILES):
                        ins = pe.transpose(gate_ps[0:TT, t * ROUTE_COLS:(t + 1) * ROUTE_COLS],
                                           route_sb[:, t * TT:(t + 1) * TT], ident[0:ROUTE_COLS, 0:ROUTE_COLS])
                    ins.then_inc(pe_turn_route, 1)

            for i in range(4):
                step(i, i % 2)
            with pe.Fori(4, GROUPS - 2, 2) as i:
                step(i, 0)
                step(i + 1, 1)
            for i in range(GROUPS - 2, GROUPS + 3):
                step(i, i % 2)


def shape_constants():
    f, t = np.arange(NF), np.arange(N_TOK)
    angle = 2 * np.pi * ((f[:, None] * t[None, :]) % N_TOK) / N_TOK
    cos, sin = np.cos(angle), np.sin(angle)
    sin[[0, HALF], :] = 0.0
    sin[:, [0, HALF]] = 0.0
    weight = np.where((f == 0) | (f == HALF), 1.0, 2.0) / N_TOK
    fwd = cos[:, :NF].copy()
    fwd[HALF] *= 0.5
    earlier = np.tril(np.ones((EXPERTS, EXPERTS)), -1) * -TINY
    c32 = lambda a: np.ascontiguousarray(a, dtype=np.float32)
    return {
        "ident": c32(np.eye(P)),
        "cos_fwd": c32(fwd),
        "sin_fwd": c32(-sin[:, :NF]),
        "cos_inv": c32(cos),
        "sin_inv": c32(-sin),
        "cos_tap": c32((weight[:, None] * cos[:, :TAPS]).T),
        "sin_tap": c32((weight[:, None] * -sin[:, :TAPS]).T),
        "rank_thr": c32(np.broadcast_to(earlier, (TT, TILES, EXPERTS, EXPERTS)).reshape(TT, -1)),
    }


def kernel(**inputs):
    import concourse.bacc as bacc
    from concourse.bass_utils import run_bass_kernel_spmd

    a = {k: np.asarray(v) for k, v in inputs.items()}
    x = a["x"].reshape(IMAGES, CHANNELS, GRID, PATCH, GRID, PATCH).transpose(0, 1, 3, 5, 2, 4)
    x = x.reshape(IMAGES, N_TOK, FLAT).reshape(GROUPS, GT, KT, P).transpose(0, 3, 2, 1)
    consts = shape_constants()
    pre = "L0_"
    columns = [a[pre + k].reshape(-1, P) for k in
               ("attn_in_b", "attn_mod_b2", "attn_out_b", "ffn_base_b", "attn_mod_b1")]
    route_column = np.zeros((1, P), np.float32)
    route_column[0, ROUTED:ROUTE_COLS] = a[pre + "ffn_router_b"]
    biases = np.concatenate([*columns, route_column]).T
    arrays = {
        "xg": x,
        "tok_w": a[pre + "tok_W"],
        "in_w": a[pre + "attn_in_w"],
        "w1": a[pre + "attn_mod_w1"],
        "w2": a[pre + "attn_mod_w2"],
        "taps_t": a[pre + "attn_kernel"].T,
        "out_w": a[pre + "attn_out_w"],
        "base_wt": a[pre + "ffn_base_W"].T,
        "shared_a": a[pre + "ffn_shared_A"],
        "shared_bt": a[pre + "ffn_shared_B"].T,
        "route_w": np.concatenate([a[pre + "ffn_routed_A"].reshape(ROUTED, DIM), a[pre + "ffn_router_W"]]).T,
        "routed_bt": a[pre + "ffn_routed_B"].transpose(0, 2, 1).reshape(ROUTED, DIM),
        "biases": biases,
        **consts,
    }
    arrays = {k: np.ascontiguousarray(v) for k, v in arrays.items()}
    nc = bacc.Bacc("TRN2", target_bir_lowering=False, num_devices=1)
    args = [nc.dram_tensor("dram_" + k, v.shape, mybir.dt.from_np(v.dtype), kind="ExternalInput").ap()
            for k, v in arrays.items()]
    out = nc.dram_tensor("out", (DIM, IMAGES * N_TOK), F32, kind="ExternalOutput").ap()
    tower_program(nc, *args, out)
    r = run_bass_kernel_spmd(nc, [{"dram_" + k: v for k, v in arrays.items()}], core_ids=[0])
    return np.ascontiguousarray(r.results[0]["out"].T).reshape(IMAGES, N_TOK, DIM)
```

```python
from contextlib import ExitStack

import numpy as np

import concourse.bass as bass
from concourse import mybir

F32 = mybir.dt.float32
F32R = mybir.dt.float32r
I32 = mybir.dt.int32
ACT = mybir.ActivationFunctionType
ALU = mybir.AluOpType
AX_X = mybir.AxisListType.X

P = 128
IMAGES, CHANNELS, SIDE, PATCH = 64, 3, 224, 16
GRID = SIDE // PATCH
N_TOK = GRID * GRID
FLAT = CHANNELS * PATCH * PATCH
DIM = 256
HID = 1024
TAPS = 64
EXPERTS, RANK = 6, 16
ROUTED = EXPERTS * RANK
ROUTE_COLS = ROUTED + EXPERTS
LN_EPS = 1e-5
GATE_EPS = 1e-6

PAIR = 2
GROUPS = IMAGES // PAIR
GT = PAIR * N_TOK
TILES = 4
TT = GT // TILES
KT = FLAT // P
DH = DIM // P
HC = HID // P
HALF = N_TOK // 2
NF = HALF + 1
NFP = NF + 1
SLOTS = 3
BANK = 512
CONSTS = 10
RSQRT_MAGIC, RSQRT_K1, RSQRT_K2 = 1595932665.0, 0.703952253, 2.38924456
TINY = 1.1754944e-38
LOG2_E, ROUND, LEAST_EXP, EXP_BIAS, EXP_UNIT = 1.4426950408889634, 1.5 * 2.0 ** 23, -87.0, 127.0, 2.0 ** 23
EXP2_POLY = (0.0001546734499, 0.001340038947, 0.009618036033,
             0.05550327361, 0.2402265108, 0.6931472066)
LOOP_END = GROUPS - 2 - SLOTS + 1

EARLY_K, LATE_K = range(KT // 2), range(KT // 2, KT)
LN_STEPS = 16
GATE_STEPS = 24
EXP_STEPS = 13


def exists(g):
    return 0 <= g < GROUPS if isinstance(g, int) else True


def tower_program(nc: bass.Bass, xg, tok_w, in_w, w1, w2, taps_t, out_w, base_wt,
                  shared_a, shared_bt, route_w, routed_bt, biases_d, ident_d, cos_fwd_d, sin_fwd_d, cos_inv_d,
                  sin_inv_d, cos_tap_d, sin_tap_d, rank_thr_d, out):
    ctx = ExitStack()
    with ctx:
        def sb(name, shape, dt=F32):
            return ctx.enter_context(nc.sbuf_tensor(name, shape, dt))

        def sem(name):
            return ctx.enter_context(nc.semaphore(name))

        def pair(name, shape):
            return sb(name + "_h", shape, F32R), sb(name + "_l", shape, F32R)

        tokw_h, tokw_l = pair("tokw", [P, KT, DIM])
        inw_h, inw_l = pair("inw", [P, DH, DIM])
        w1_h, w1_l = pair("w1", [P, DH, HID])
        w2_h, w2_l = pair("w2", [P, HC, DIM])
        outw_h, outw_l = pair("outw", [P, DH, DIM])
        route_h, route_l = pair("route", [P, DH, ROUTE_COLS])
        base_h, base_l = pair("base", [P, DH, DIM])
        routedb_h, routedb_l = pair("routedb", [ROUTED, DIM])
        dft_h, dft_l = pair("dft", [NF, 2, 100])
        cos_inv = sb("cos_inv", [NF, N_TOK])
        sin_inv = sb("sin_inv", [NF, N_TOK])
        spec_k = sb("spec_k", [NF, 2, PAIR * DIM])
        ident = sb("ident", [P, P])
        rank_thr = sb("rank_thr", [TT, TILES * EXPERTS * EXPERTS])
        biases = sb("biases", [P, 4 * DH + HC + 1])
        in_bias = biases[:, 0:DH]
        b2_bias = biases[:, DH:2 * DH]
        out_bias = biases[:, 2 * DH:3 * DH]
        base_bias = biases[:, 3 * DH:4 * DH]
        b1_bias = biases[:, 4 * DH:4 * DH + HC]
        route_bias = biases[0:ROUTE_COLS, 4 * DH + HC:4 * DH + HC + 1]

        patches = sb("patches", [P, KT, GT])
        patches_h, patches_l = pair("patches", [P, KT, GT])
        h_sb = sb("h_sb", [P, SLOTS, DH, GT])
        norm1 = sb("norm1", [TT, TILES, DIM])
        norm2 = sb("norm2", [TT, TILES, DIM])
        x1_h, x1_l = pair("x1", [P, DH, GT])
        x2_h, x2_l = pair("x2", [P, DH, GT])
        x_proj = sb("x_proj", [P, DH, GT])
        gelu = sb("gelu", [P, 4, GT])
        gelu_h, gelu_l = pair("gelu", [P, HC, GT])
        modulated = sb("modulated", [P, DH, PAIR, N_TOK])
        folded = sb("folded", [P, DH, 2, PAIR, NFP])
        fold_h, fold_l = pair("fold", [NF, 2, PAIR * DIM])
        prod = sb("prod", [P, 2, 2, PAIR * DIM])
        spec_y = sb("spec_y", [NF, 2, PAIR * DIM])
        y_h, y_l = pair("y", [P, DH, GT])
        route_sb = sb("route_sb", [ROUTE_COLS, GT])
        gated = sb("gated", [TT, TILES, ROUTED])
        gated_h, gated_l = pair("gated", [ROUTED, GT])
        result = sb("result", [P, DH, GT])
        stage = prod[:, :, :, :].rearrange("p a b n -> p (a b n)")
        taps = sb("taps", [TAPS, DIM])
        tap_mats = sb("tap_mats", [TAPS, 2, 100])
        shared_sb = sb("shared_sb", [RANK, 2 * DIM])
        bn = sb("bn", [TT, 2, TILES, 6])
        mean_var = sb("mean_var", [TT, 2, TILES, 2])
        ln_tmp = sb("ln_tmp", [TT, 15, 2, TILES])
        gate_small = sb("gate_small", [TT, 8, TILES])
        gate_wide = sb("gate_wide", [TT, 11, TILES, EXPERTS])
        gate_cmp = sb("gate_cmp", [TT, 2, TILES, EXPERTS, EXPERTS])

        big = [ctx.enter_context(nc.psum_tensor(f"big{n}", [P, BANK], F32)) for n in range(3)]
        turn = ctx.enter_context(nc.psum_tensor("turn", [P, 2, BANK], F32))
        turn2 = ctx.enter_context(nc.psum_tensor("turn2", [P, 2, BANK], F32))
        IN_BANK, UP_BANK, FFN_BANK = (0, 1), (2, 0, 1, 2, 0, 1, 1, 2), (2, 0)
        EMBED_BANK, OUT_BANK, DOWN_BANK = (0, 1), (2, 0), (1, 2)
        gate_ps = ctx.enter_context(nc.psum_tensor("gate_ps", [P, BANK], F32))

        weight_in = [sem(f"weight_in{n}") for n in range(9)]
        const_in = sem("const_in")
        patches_in = sem("patches_in")
        result_out = sem("result_out")
        pad_zero = sem("pad_zero")
        weight_hi = sem("weight_hi")
        weight_lo = sem("weight_lo")
        setup_mm = sem("setup_mm")
        spectrum_ready = sem("spectrum_ready")
        base_sum = sem("base_sum")
        pe_embed = sem("pe_embed")
        pe_turn_h = sem("pe_turn_h")
        pe_turn_x1 = sem("pe_turn_x1")
        pe_in = sem("pe_in")
        pe_w1 = sem("pe_w1")
        pe_w2 = sem("pe_w2")
        pe_turn_fold = sem("pe_turn_fold")
        pe_dft = sem("pe_dft")
        pe_idft = sem("pe_idft")
        pe_out = sem("pe_out")
        pe_turn_h2 = sem("pe_turn_h2")
        pe_turn_x2 = sem("pe_turn_x2")
        pe_route = sem("pe_route")
        pe_turn_route = sem("pe_turn_route")
        pe_turn_gated = sem("pe_turn_gated")
        pe_ffn = sem("pe_ffn")
        act_patches_hi = sem("act_patches_hi")
        act_h = sem("act_h")
        act_norm1 = sem("act_norm1")
        act_x1_hi = sem("act_x1_hi")
        act_in = sem("act_in")
        act_gelu = sem("act_gelu")
        act_gelu_hi = sem("act_gelu_hi")
        act_fold_hi = sem("act_fold_hi")
        act_y_hi = sem("act_y_hi")
        act_norm2 = sem("act_norm2")
        act_x2_hi = sem("act_x2_hi")
        act_route = sem("act_route")
        act_gated_hi = sem("act_gated_hi")
        dve_ln = sem("dve_ln")
        dve_norm1 = sem("dve_norm1")
        dve_norm2 = sem("dve_norm2")
        dve_x1_lo = sem("dve_x1_lo")
        dve_gelu_lo = sem("dve_gelu_lo")
        dve_mod = sem("dve_mod")
        dve_fold_lo = sem("dve_fold_lo")
        dve_spec = sem("dve_spec")
        dve_y_lo = sem("dve_y_lo")
        dve_h2 = sem("dve_h2")
        dve_x2_lo = sem("dve_x2_lo")
        dve_gate = sem("dve_gate")
        gate_done = sem("gate_done")
        dve_gated_lo = sem("dve_gated_lo")
        dve_result = sem("dve_result")
        pool_patches_lo = sem("pool_patches_lo")
        pool_fold = sem("pool_fold")

        out_v = out.rearrange("(m p) t -> p m t", p=P)

        gh = gelu[:, :, :].rearrange("p k t -> p (k t)")
        splits = [
            (tok_w.rearrange("(k p) n -> p k n", p=P), stage[:, 0:KT * DIM], tokw_h, tokw_l),
            (in_w.rearrange("(k p) n -> p k n", p=P), gh[:, 0:DH * DIM], inw_h, inw_l),
            (out_w.rearrange("(k p) n -> p k n", p=P), gh[:, DH * DIM:2 * DH * DIM], outw_h, outw_l),
            (route_w.rearrange("(k p) n -> p k n", p=P), gh[:, 2 * DH * DIM:2 * DH * DIM + DH * ROUTE_COLS],
             route_h, route_l),
            (routed_bt, norm2[0:ROUTED, 0, :], routedb_h, routedb_l),
            (w1.rearrange("(k p) n -> p k n", p=P), stage, w1_h, w1_l),
            (w2.rearrange("(k p) n -> p k n", p=P), stage, w2_h, w2_l),
        ]

        block = ctx.enter_context(nc.Block())

        @block.sync
        def _(sp):
            def const(dst, src):
                sp.dma_start(dst, src).then_inc(const_in, 16)

            sp.dma_start(stage[:, 0:KT * DIM].rearrange("p (k n) -> p k n", k=KT), splits[0][0])\
                .then_inc(weight_in[0], 16)
            sp.dma_start(patches[:, :, :], xg[0]).then_inc(patches_in, 16)
            const(ident[:, :], ident_d)
            for n in range(1, 5):
                src, dst = splits[n][0], splits[n][1]
                if n < 4:
                    dst = dst.rearrange("p (k n) -> p k n", k=DH)
                sp.dma_start(dst, src).then_inc(weight_in[n], 16)
            sp.dma_start(spec_y[:, 0, 0:NF], cos_fwd_d).then_inc(weight_in[7], 16)
            sp.dma_start(spec_y[:, 1, 0:NF], sin_fwd_d).then_inc(weight_in[7], 16)
            sp.dma_start(x_proj[:, :, 0:DIM], base_wt.rearrange("(k p) n -> p k n", p=P)).then_inc(weight_in[8], 16)
            const(biases[:, :], biases_d)
            const(taps[:, :], taps_t)
            const(tap_mats[:, 0, 0:NF], cos_tap_d)
            const(tap_mats[:, 1, 0:NF], sin_tap_d)
            const(cos_inv[:, :], cos_inv_d)
            const(sin_inv[:, :], sin_inv_d)
            const(shared_sb[:, 0:DIM], shared_a)
            const(shared_sb[:, DIM:2 * DIM], shared_bt)
            const(rank_thr[:, :], rank_thr_d)
            for n, k in ((5, DH), (6, HC)):
                sp.wait_ge(weight_lo, 1 if n == 5 else 7)
                sp.dma_start(stage.rearrange("p (k n) -> p k n", k=k), splits[n][0])\
                    .then_inc(weight_in[n], 16)

            def step(i):
                front, tail = i, i - 3
                if exists(tail):
                    sp.wait_ge(dve_result, 2 * tail + 2)
                    sp.dma_start(out_v[:, :, bass.ds(tail * GT, GT)], result[:, :, :]).then_inc(result_out, 16)
                if exists(front) and (not isinstance(front, int) or front + 1 < GROUPS):
                    sp.wait_ge(pool_patches_lo, KT * front + KT)
                    sp.dma_start(patches[:, :, :], xg[bass.ds(front + 1, 1)].rearrange("g p k t -> p (g k) t"))\
                        .then_inc(patches_in, 16)

            for i in range(3):
                step(i)
            with sp.Fori(3, LOOP_END, SLOTS) as i:
                for slot in range(SLOTS):
                    step(i + slot)
            for i in range(GROUPS - 2, GROUPS + 3):
                step(i)
            sp.wait_ge(result_out, 16 * GROUPS)

        @block.gpsimd
        def _(pool):
            pool.memset(folded[:, :, :, :, :], 0.0).then_inc(pad_zero, 1)

            def patches_lo(g, ks):
                for k in ks:
                    pool.wait_ge(act_patches_hi, KT * g + k + 1)
                    pool.tensor_tensor(patches_l[:, k, :], patches[:, k, :], patches_h[:, k, :].bitcast(F32),
                                       ALU.subtract).then_inc(pool_patches_lo, 1)

            def fold(g):
                for m in range(DH):
                    pool.wait_ge(dve_mod, DH * g + m + 1)
                    if m == 0:
                        if exists(g - 1):
                            pool.wait_ge(pe_turn_fold, g)
                        else:
                            pool.wait_ge(pad_zero, 1)
                    fwd = modulated[:, m, :, 1:NF]
                    back = modulated[:, m, :, N_TOK - 1:N_TOK - NF:-1]
                    pool.tensor_tensor(folded[:, m, 0, :, 1:NF], fwd, back, ALU.add)
                    pool.tensor_copy(folded[:, m, 0, :, 0:1], modulated[:, m, :, 0:1])
                    pool.tensor_tensor(folded[:, m, 1, :, 1:NF], fwd, back, ALU.subtract).then_inc(pool_fold, 1)

            def step(i):
                front, mid = i, i - 1
                if exists(front):
                    patches_lo(front, range(KT) if isinstance(i, int) and i == 0 else LATE_K)
                if exists(front + 1):
                    patches_lo(front + 1, EARLY_K)
                if exists(mid):
                    fold(mid)

            for i in range(3):
                step(i)
            with pool.Fori(3, LOOP_END, SLOTS) as i:
                for slot in range(SLOTS):
                    step(i + slot)
            for i in range(GROUPS - 2, GROUPS + 3):
                step(i)

        @block.scalar
        def _(act):
            def weight_split(n):
                src, stage_ap, hi, lo = splits[n]
                act.wait_ge(weight_in[n], 16)
                flat = hi[:, :] if len(hi.shape) == 2 else hi[:, :, :].rearrange("p k n -> p (k n)")
                act.activation(flat, stage_ap, ACT.Copy).then_inc(weight_hi, 1)

            def patches_hi(g, ks):
                for k in ks:
                    if k == 0:
                        act.wait_ge(patches_in, 16 * (g + 1))
                        if exists(g - 1):
                            act.wait_ge(pe_embed, DH * g)
                    act.activation(patches_h[:, k, :], patches[:, k, :], ACT.Copy).then_inc(act_patches_hi, 1)

            weight_split(0)
            patches_hi(0, range(KT))
            act.wait_ge(weight_in[7], 32)
            act.activation(dft_h[:, :, 0:NF], spec_y[:, :, 0:NF], ACT.Copy).then_inc(weight_hi, 1)
            for n in (1, 2, 3, 4, 5, 6):
                weight_split(n)
            act.wait_ge(base_sum, DH)
            act.activation(base_h[:, :, :], x_proj[:, :, 0:DIM], ACT.Copy).then_inc(weight_hi, 1)
            act.wait_ge(const_in, 16 * CONSTS)

            def normalise(norm, which, ps, signal):
                for t in range(TILES // 2):
                    ins = act.activation(norm[:, t, :], ps[0:TT, 0, DIM * t:DIM * t + DIM], ACT.Identity,
                                         bias=ln_tmp[:, 1, which, t:t + 1], scale=ln_tmp[:, 0, which, t:t + 1])
                ins.then_inc(signal, 1)

            def step(i, slot):
                front, mid, back, tail = i, i - 1, i - 2, i - 3

                def gelu_tile(k):
                    act.wait_ge(pe_w1, HC * mid + k + 1)
                    if k % 2 == 0:
                        if k >= 4:
                            act.wait_ge(dve_gelu_lo, 4 * mid + k // 2 - 1)
                        elif exists(mid - 1):
                            act.wait_ge(dve_gelu_lo, 4 * (mid - 1) + k // 2 + 3)
                    act.activation(gelu[:, k % 4, :], big[UP_BANK[k]][:, 0:GT], ACT.Gelu,
                                   bias=b1_bias[:, k:k + 1]).then_inc(act_gelu, 1)

                def gelu_hi(j):
                    act.wait_ge(act_gelu, HC * mid + 2 * j + 2)
                    s = (2 * j) % 4
                    act.activation(gelu_h[:, 2 * j:2 * j + 2, :], gelu[:, s:s + 2, :], ACT.Copy)\
                        .then_inc(act_gelu_hi, 1)

                if exists(mid):
                    for m in range(DH):
                        act.wait_ge(pe_in, DH * mid + m + 1)
                        if m == 0:
                            if exists(mid - 1):
                                act.wait_ge(dve_mod, DH * mid)
                            else:
                                act.wait_ge(weight_lo, 9)
                        act.activation(x_proj[:, m, :], big[IN_BANK[m]][:, 0:GT], ACT.Identity,
                                       bias=in_bias[:, m:m + 1]).then_inc(act_in, 1)
                if exists(tail):
                    act.wait_ge(pe_route, tail + 1)
                    act.activation(route_sb[:, :], gate_ps[0:ROUTE_COLS, 0:GT], ACT.Identity,
                                   bias=route_bias).then_inc(act_route, 1)
                if exists(mid):
                    gelu_tile(0)
                if exists(back):
                    act.wait_ge(pe_turn_fold, back + 1)
                    act.activation(fold_h[:, :, :], turn[0:NF, :, :], ACT.Copy).then_inc(act_fold_hi, 1)
                if exists(mid):
                    gelu_tile(1)
                    gelu_hi(0)
                    gelu_tile(2)
                    gelu_tile(3)
                    gelu_hi(1)
                    gelu_tile(4)
                    gelu_tile(5)
                if exists(tail):
                    act.wait_ge(pe_turn_gated, tail + 1)
                    act.activation(gated_h[:, :], gate_ps[0:ROUTED, 0:GT], ACT.Copy).then_inc(act_gated_hi, 1)
                if exists(mid):
                    gelu_hi(2)
                if exists(front) and not (isinstance(i, int) and i == 0):
                    patches_hi(front, LATE_K)
                if exists(mid):
                    gelu_tile(6)
                    gelu_tile(7)
                    gelu_hi(3)
                if exists(back):
                    act.wait_ge(pe_idft, back + 1)
                    act.activation(y_h[:, :, :], turn[:, :, 0:GT], ACT.Copy).then_inc(act_y_hi, 1)
                if exists(front):
                    if exists(tail):
                        act.wait_ge(dve_result, DH * tail + 2)
                    for m in range(DH):
                        act.wait_ge(pe_embed, DH * front + m + 1)
                        act.activation(h_sb[:, slot, m, :], big[EMBED_BANK[m]][:, 0:GT], ACT.Copy)\
                            .then_inc(act_h, 1)
                if exists(front) or exists(back):
                    act.wait_ge(dve_ln, LN_STEPS * i + LN_STEPS)
                if exists(front):
                    normalise(norm1, 0, turn, act_norm1)
                if exists(back):
                    normalise(norm2, 1, turn2, act_norm2)
                if exists(front):
                    act.wait_ge(pe_turn_x1, DH * front + DH)
                    act.activation(x1_h[:, :, :], turn[:, :, 0:GT], ACT.Copy).then_inc(act_x1_hi, 1)
                if exists(front + 1):
                    patches_hi(front + 1, EARLY_K)
                if exists(back):
                    for m in range(DH):
                        act.wait_ge(pe_turn_x2, DH * back + m + 1)
                        act.activation(x2_h[:, m, :], turn2[:, m, 0:GT], ACT.Copy).then_inc(act_x2_hi, 1)

            for i in range(3):
                step(i, i)
            with act.Fori(3, LOOP_END, SLOTS) as i:
                for slot in range(SLOTS):
                    step(i + slot, slot)
            for i in range(GROUPS - 2, GROUPS + 3):
                step(i, i % SLOTS)

        @block.vector
        def _(dve):
            def weight_split(n, order):
                src, stage_ap, hi, lo = splits[n]
                dve.wait_ge(weight_hi, order)
                if len(hi.shape) == 2:
                    h, l = hi[:, :], lo[:, :]
                else:
                    h, l = (w[:, :, :].rearrange("p k n -> p (k n)") for w in (hi, lo))
                dve.tensor_tensor(l, stage_ap, h.bitcast(F32), ALU.subtract).then_inc(weight_lo, 1)

            weight_split(0, 1)
            dve.wait_ge(weight_hi, 2)
            dve.tensor_tensor(dft_l[:, :, 0:NF], spec_y[:, :, 0:NF], dft_h[:, :, 0:NF].bitcast(F32),
                              ALU.subtract).then_inc(weight_lo, 1)
            for order, n in enumerate((1, 2, 3, 4)):
                weight_split(n, order + 3)
            weight_split(5, 7)
            dve.wait_ge(setup_mm, 2 + DH)
            for img in range(PAIR):
                ins = dve.tensor_copy(spec_k[:, :, img * DIM:(img + 1) * DIM], turn2[0:NF, :, 0:DIM])
            ins.then_inc(spectrum_ready, 1)
            dve.wait_ge(weight_in[8], 16)
            for k in range(DH):
                dve.tensor_tensor(x_proj[:, k, 0:DIM], turn2[:, k, DIM:2 * DIM], x_proj[:, k, 0:DIM], ALU.add)\
                    .then_inc(base_sum, 1)
            weight_split(6, 8)
            dve.wait_ge(weight_hi, 9)
            dve.tensor_tensor(base_l[:, :, :], x_proj[:, :, 0:DIM], base_h[:, :, :].bitcast(F32), ALU.subtract)\
                .then_inc(weight_lo, 1)
            dve.wait_ge(const_in, 16 * CONSTS)

            def bn_stats(g, which, ps, ready):
                for t in range(TILES):
                    if t % 2 == 0:
                        dve.wait_ge(ready, 2 * g + t // 2 + 1)
                    ins = dve.bn_stats(bn[:, which, t, :], ps[0:TT, t // 2, DIM * (t % 2):DIM * (t % 2) + DIM])
                return ins

            def layer_norm_scales(i, stats, norms):
                done = [0]
                tmp = lambda n: ln_tmp[:, n, norms, :]

                def link(ins, wait=True):
                    done[0] += 1
                    ins.then_inc(dve_ln, 1)
                    if wait:
                        dve.wait_ge(dve_ln, LN_STEPS * i + done[0])

                link(stats)
                mean_m2 = mean_var[:, norms]
                link(dve.tensor_reduce(mean_m2, bn[:, norms].rearrange("p w t (x f) -> p w t f x", x=2)
                                       [:, :, :, 1:3, :], AX_X, ALU.add), wait=False)
                diff, within, between = tmp(12), tmp(13), tmp(14)
                link(dve.tensor_tensor(diff, bn[:, norms, :, 1], bn[:, norms, :, 4], ALU.subtract))
                link(dve.tensor_scalar(within, mean_m2[:, :, :, 1], 1.0 / DIM, LN_EPS, ALU.mult, ALU.add),
                     wait=False)
                link(dve.scalar_tensor_tensor(out=between, in0=diff, scalar=0.25, in1=diff, op0=ALU.mult,
                                              op1=ALU.mult))
                v = tmp(2)
                link(dve.tensor_tensor(v, within, between, ALU.add))
                guess, r1, r = tmp(3), tmp(6), tmp(0)
                link(dve.tensor_scalar(guess.bitcast(I32), v.bitcast(I32), -0.5, RSQRT_MAGIC, ALU.mult, ALU.add))
                link(dve.tensor_tensor(tmp(4), guess, guess, ALU.mult))
                link(dve.scalar_tensor_tensor(out=tmp(5), in0=tmp(4), scalar=-RSQRT_K1, in1=v, op0=ALU.mult,
                                              op1=ALU.mult))
                link(dve.scalar_tensor_tensor(out=r1, in0=tmp(5), scalar=RSQRT_K1 * RSQRT_K2, in1=guess,
                                              op0=ALU.add, op1=ALU.mult))
                link(dve.tensor_scalar(tmp(7), r1, 0.375, None, ALU.mult), wait=False)
                link(dve.tensor_tensor(tmp(8), r1, r1, ALU.mult))
                link(dve.tensor_tensor(tmp(9), tmp(8), v, ALU.mult))
                link(dve.scalar_tensor_tensor(out=tmp(10), in0=tmp(9), scalar=-10.0 / 3.0, in1=tmp(9),
                                              op0=ALU.add, op1=ALU.mult))
                link(dve.scalar_tensor_tensor(out=r, in0=tmp(10), scalar=5.0, in1=tmp(7), op0=ALU.add,
                                              op1=ALU.mult))
                link(dve.scalar_tensor_tensor(out=tmp(1), in0=mean_m2[:, :, :, 0], scalar=-0.5, in1=r,
                                              op0=ALU.mult, op1=ALU.mult))
                assert done[0] == LN_STEPS

            def normalise(norm, which, ps, signal):
                for t in range(TILES // 2, TILES):
                    c = DIM * (t - TILES // 2)
                    ins = dve.tensor_scalar(norm[:, t, :], ps[0:TT, 1, c:c + DIM], ln_tmp[:, 0, which, t:t + 1],
                                            ln_tmp[:, 1, which, t:t + 1], ALU.mult, ALU.add)
                ins.then_inc(signal, 1)

            def over_experts(a):
                return a.rearrange("p (t a) -> p t a", a=1).broadcast_to([TT, TILES, EXPERTS])

            rows = gate_ps[0:TT, 0:TILES * ROUTE_COLS].rearrange("p (t c) -> p t c", t=TILES)
            small = lambda n: gate_small[:, n, :]
            wide = lambda n: gate_wide[:, n].rearrange("p t e -> p (t e)")

            def gate_exp(g):
                done = [0]

                def link(ins, wait=True):
                    done[0] += 1
                    ins.then_inc(dve_gate, 1)
                    if wait:
                        dve.wait_ge(dve_gate, GATE_STEPS * g + done[0])

                logits = rows[:, :, ROUTED:ROUTE_COLS]
                dve.wait_ge(pe_turn_route, g + 1)
                link(dve.tensor_reduce(small(0), logits, AX_X, ALU.max))
                link(dve.tensor_tensor(gate_wide[:, 0], logits, over_experts(small(0)), ALU.subtract))
                scaled, whole, part, power, poly = (wide(n) for n in range(6, 11))
                link(dve.tensor_scalar(scaled, wide(0), LEAST_EXP, LOG2_E, ALU.max, ALU.mult))
                link(dve.tensor_scalar(whole, scaled, ROUND, ROUND, ALU.add, ALU.subtract))
                link(dve.tensor_tensor(part, scaled, whole, ALU.subtract), wait=False)
                link(dve.tensor_scalar(power.bitcast(I32), whole, EXP_BIAS, EXP_UNIT, ALU.add, ALU.mult))
                link(dve.tensor_scalar(poly, part, EXP2_POLY[0], None, ALU.mult))
                for coef in EXP2_POLY[1:]:
                    link(dve.scalar_tensor_tensor(out=poly, in0=poly, scalar=coef, in1=part, op0=ALU.add,
                                                  op1=ALU.mult))
                link(dve.scalar_tensor_tensor(out=wide(1), in0=poly, scalar=1.0, in1=power, op0=ALU.add,
                                              op1=ALU.mult), wait=False)
                assert done[0] == EXP_STEPS

            def gate(g):
                done = [EXP_STEPS]

                def link(ins):
                    done[0] += 1
                    ins.then_inc(dve_gate, 1)
                    dve.wait_ge(dve_gate, GATE_STEPS * g + done[0])

                dve.wait_ge(dve_gate, GATE_STEPS * g + EXP_STEPS)
                link(dve.tensor_reduce(small(1), gate_wide[:, 1], AX_X, ALU.add))
                link(dve.reciprocal(small(2), small(1)))
                gates = gate_wide[:, 2]
                link(dve.tensor_tensor(gates, gate_wide[:, 1], over_experts(small(2)), ALU.mult))
                e4 = [TT, TILES, EXPERTS, EXPERTS]
                other = gates.rearrange("p t (a e) -> p t a e", a=1).broadcast_to(e4)
                own = gates.rearrange("p t (e a) -> p t e a", a=1).broadcast_to(e4)
                link(dve.tensor_tensor(gate_cmp[:, 0], other, own, ALU.subtract))
                flat = lambda n: gate_cmp[:, n].rearrange("p t e f -> p (t e f)")
                link(dve.tensor_tensor(flat(1), flat(0), rank_thr[:, :], ALU.is_gt))
                link(dve.tensor_reduce(gate_wide[:, 3], gate_cmp[:, 1], AX_X, ALU.add))
                link(dve.scalar_tensor_tensor(out=wide(4), in0=wide(3), scalar=1.5, in1=wide(2), op0=ALU.is_lt,
                                              op1=ALU.mult))
                link(dve.tensor_reduce(small(3), gate_wide[:, 4], AX_X, ALU.add))
                link(dve.tensor_scalar(small(4), small(3), GATE_EPS, None, ALU.add))
                link(dve.reciprocal(small(5), small(4)))
                link(dve.tensor_tensor(gate_wide[:, 5], gate_wide[:, 4], over_experts(small(5)), ALU.mult))
                assert done[0] == GATE_STEPS
                hidden = rows[:, :, 0:ROUTED].rearrange("p t (e r) -> p t e r", r=RANK)
                weight = gate_wide[:, 5].rearrange("p t (e a) -> p t e a", a=1)\
                    .broadcast_to([TT, TILES, EXPERTS, RANK])
                dve.tensor_tensor(gated[:, :, :].rearrange("p t (e r) -> p t e r", r=RANK), hidden, weight,
                                  ALU.mult).then_inc(gate_done, 1)

            def gelu_lo(g, j):
                dve.wait_ge(act_gelu_hi, 4 * g + j + 1)
                s = (2 * j) % 4
                dve.tensor_tensor(gelu_l[:, 2 * j:2 * j + 2, :], gelu[:, s:s + 2, :],
                                  gelu_h[:, 2 * j:2 * j + 2, :].bitcast(F32), ALU.subtract).then_inc(dve_gelu_lo, 1)

            def step(i, slot):
                front, mid, back, tail = i, i - 1, i - 2, i - 3

                def modulate(m):
                    dve.wait_ge(pe_w2, DH * mid + m + 1)
                    dve.wait_ge(act_in, DH * mid + m + 1)
                    if exists(mid - 1):
                        dve.wait_ge(pool_fold, DH * (mid - 1) + m + 1)
                    dve.scalar_tensor_tensor(out=modulated[:, m, :, :].rearrange("p a t -> p (a t)"),
                                             in0=big[DOWN_BANK[m]][:, 0:GT], scalar=b2_bias[:, m:m + 1],
                                             in1=x_proj[:, m, :], op0=ALU.add, op1=ALU.mult).then_inc(dve_mod, 1)

                def finish(m):
                    dve.wait_ge(pe_ffn, DH * tail + m + 1)
                    if m == 0 and exists(tail - 1):
                        dve.wait_ge(result_out, 16 * tail)
                    dve.scalar_tensor_tensor(out=result[:, m, :], in0=big[FFN_BANK[m]][:, 0:GT],
                                             scalar=base_bias[:, m:m + 1], in1=h_sb[:, slot, m, :], op0=ALU.add,
                                             op1=ALU.add).then_inc(dve_result, 1)

                if exists(tail):
                    gate_exp(tail)
                if exists(back):
                    dve.wait_ge(act_fold_hi, back + 1)
                    dve.tensor_tensor(fold_l[:, :, :], turn[0:NF, :, :], fold_h[:, :, :].bitcast(F32),
                                      ALU.subtract).then_inc(dve_fold_lo, 1)
                if exists(mid):
                    gelu_lo(mid, 0)
                if exists(tail):
                    gate(tail)
                if exists(mid):
                    gelu_lo(mid, 1)
                if exists(tail):
                    dve.wait_ge(act_gated_hi, tail + 1)
                    dve.tensor_tensor(gated_l[:, :], gate_ps[0:ROUTED, 0:GT], gated_h[:, :].bitcast(F32),
                                      ALU.subtract).then_inc(dve_gated_lo, 1)
                if exists(back):
                    dve.wait_ge(pe_dft, back + 1)
                    for x in range(2):
                        dve.tensor_tensor(prod[0:NF, 0, x, :], turn[0:NF, x, :], spec_k[:, 0, :], ALU.mult)
                if exists(tail):
                    finish(0)
                    finish(1)
                if exists(back):
                    for x in range(2):
                        ins = dve.tensor_tensor(prod[0:NF, 1, x, :], turn[0:NF, x, :], spec_k[:, 1, :], ALU.mult)
                    ins.then_inc(dve_spec, 1)
                    dve.wait_ge(dve_spec, 3 * back + 1)
                    dve.tensor_tensor(spec_y[:, 0, :], prod[0:NF, 0, 0, :], prod[0:NF, 1, 1, :], ALU.subtract)\
                        .then_inc(dve_spec, 1)
                    dve.tensor_tensor(spec_y[:, 1, :], prod[0:NF, 0, 1, :], prod[0:NF, 1, 0, :], ALU.add)\
                        .then_inc(dve_spec, 1)
                if exists(mid):
                    gelu_lo(mid, 2)
                    gelu_lo(mid, 3)
                if exists(back):
                    back_slot = (slot + 1) % SLOTS
                    dve.wait_ge(act_y_hi, back + 1)
                    dve.tensor_tensor(y_l[:, :, :], turn[:, :, 0:GT], y_h[:, :, :].bitcast(F32), ALU.subtract)\
                        .then_inc(dve_y_lo, 1)
                    for m in range(DH):
                        dve.wait_ge(pe_out, DH * back + m + 1)
                        dve.scalar_tensor_tensor(out=h_sb[:, back_slot, m, :], in0=big[OUT_BANK[m]][:, 0:GT],
                                                 scalar=out_bias[:, m:m + 1], in1=h_sb[:, back_slot, m, :],
                                                 op0=ALU.add, op1=ALU.add).then_inc(dve_h2, 1)
                if exists(front):
                    stats = bn_stats(front, 0, turn, pe_turn_h)
                if exists(back):
                    stats = bn_stats(back, 1, turn2, pe_turn_h2)
                if exists(front) or exists(back):
                    layer_norm_scales(i, stats, slice(0 if exists(front) else 1, 2 if exists(back) else 1))
                if exists(front):
                    normalise(norm1, 0, turn, dve_norm1)
                if exists(back):
                    normalise(norm2, 1, turn2, dve_norm2)
                if exists(front):
                    dve.wait_ge(act_x1_hi, front + 1)
                    dve.tensor_tensor(x1_l[:, :, :], turn[:, :, 0:GT], x1_h[:, :, :].bitcast(F32), ALU.subtract)\
                        .then_inc(dve_x1_lo, 1)
                if exists(mid):
                    modulate(0)
                    modulate(1)
                if exists(back):
                    for m in range(DH):
                        dve.wait_ge(act_x2_hi, DH * back + m + 1)
                        dve.tensor_tensor(x2_l[:, m, :], turn2[:, m, 0:GT], x2_h[:, m, :].bitcast(F32),
                                          ALU.subtract).then_inc(dve_x2_lo, 1)

            for i in range(3):
                step(i, i)
            with dve.Fori(3, LOOP_END, SLOTS) as i:
                for slot in range(SLOTS):
                    step(i + slot, slot)
            for i in range(GROUPS - 2, GROUPS + 3):
                step(i, i % SLOTS)

        @block.tensor
        def _(pe):
            def mm3(ps, w_h, w_l, x_h, x_l, first, last):
                pe.matmul(ps, w_h, x_h, start=first, stop=False)
                pe.matmul(ps, w_h, x_l, start=False, stop=False)
                return pe.matmul(ps, w_l, x_h, start=False, stop=last)

            def embed(g, m):
                for k in range(KT):
                    if m == 0:
                        pe.wait_ge(pool_patches_lo, KT * g + k + 1)
                    ins = mm3(big[EMBED_BANK[m]][:, 0:GT], tokw_h[:, k, m * P:(m + 1) * P],
                              tokw_l[:, k, m * P:(m + 1) * P], patches_h[:, k, :], patches_l[:, k, :],
                              k == 0, k == KT - 1)
                ins.then_inc(pe_embed, 1)

            def to_tokens(ps, rows, signal):
                for t in range(TILES):
                    for m in range(DH):
                        c = DIM * (t % 2) + m * P
                        ins = pe.transpose(ps[0:TT, t // 2, c:c + P], rows[:, m, t * TT:(t + 1) * TT], ident[:, :])
                    if t % 2 == 1:
                        ins.then_inc(signal, 1)

            def to_features(ps, rows, signal):
                for m in range(DH):
                    for t in range(TILES):
                        ins = pe.transpose(ps[:, m, t * TT:(t + 1) * TT], rows[:, t, m * P:(m + 1) * P],
                                           ident[0:TT, 0:TT])
                    ins.then_inc(signal, 1)

            def mlp_up(g, k, cs=range(DH)):
                for c in cs:
                    ins = mm3(big[UP_BANK[k]][:, 0:GT], w1_h[:, c, k * P:(k + 1) * P],
                              w1_l[:, c, k * P:(k + 1) * P], x1_h[:, c, :], x1_l[:, c, :], c == 0, c == DH - 1)
                if cs[-1] == DH - 1:
                    ins.then_inc(pe_w1, 1)

            def mlp_down(g, m, cs):
                for c in cs:
                    if m == 0 and c % 2 == 0:
                        pe.wait_ge(dve_gelu_lo, 4 * g + c // 2 + 1)
                    ins = mm3(big[DOWN_BANK[m]][:, 0:GT], w2_h[:, c, m * P:(m + 1) * P],
                              w2_l[:, c, m * P:(m + 1) * P], gelu_h[:, c, :], gelu_l[:, c, :],
                              c == 0, c == HC - 1)
                if cs[-1] == HC - 1:
                    ins.then_inc(pe_w2, 1)

            pe.wait_ge(const_in, 16 * CONSTS)
            for c in range(2):
                pe.matmul(turn2[0:NF, c, 0:DIM], tap_mats[:, c, 0:NF], taps[:, :], start=True, stop=True)\
                    .then_inc(setup_mm, 1)
            for k in range(DH):
                pe.matmul(turn2[:, k, DIM:2 * DIM], shared_sb[:, k * P:(k + 1) * P], shared_sb[:, DIM:2 * DIM],
                          start=True, stop=True).then_inc(setup_mm, 1)

            def step(i, slot):
                front, mid, back, tail = i, i - 1, i - 2, i - 3
                if exists(mid):
                    if not exists(mid - 1):
                        pe.wait_ge(weight_lo, 7)
                    pe.wait_ge(dve_x1_lo, mid + 1)
                    for m in range(DH):
                        if m == 1 and exists(back):
                            pe.wait_ge(dve_mod, DH * back + 1)
                        for c in range(DH):
                            ins = mm3(big[IN_BANK[m]][:, 0:GT], inw_h[:, c, m * P:(m + 1) * P],
                                      inw_l[:, c, m * P:(m + 1) * P], x1_h[:, c, :], x1_l[:, c, :],
                                      c == 0, c == DH - 1)
                        ins.then_inc(pe_in, 1)
                if exists(tail):
                    for c in range(DH):
                        pe.wait_ge(dve_x2_lo, DH * tail + c + 1)
                        ins = mm3(gate_ps[0:ROUTE_COLS, 0:GT], route_h[:, c, :], route_l[:, c, :], x2_h[:, c, :],
                                  x2_l[:, c, :], c == 0, c == DH - 1)
                    ins.then_inc(pe_route, 1)
                if exists(mid):
                    if exists(back):
                        pe.wait_ge(dve_mod, DH * back + 2)
                    mlp_up(mid, 0)
                if exists(tail):
                    pe.wait_ge(act_route, tail + 1)
                    for t in range(TILES):
                        ins = pe.transpose(gate_ps[0:TT, t * ROUTE_COLS:(t + 1) * ROUTE_COLS],
                                           route_sb[:, t * TT:(t + 1) * TT], ident[0:ROUTE_COLS, 0:ROUTE_COLS])
                    ins.then_inc(pe_turn_route, 1)
                if exists(back):
                    pe.wait_ge(pool_fold, DH * back + 2)
                    for x in range(2):
                        for img in range(PAIR):
                            for m in range(DH):
                                c = img * DIM + m * P
                                ins = pe.transpose(turn[0:NFP, x, c:c + P], folded[:, m, x, img, :], ident[:, :])
                    ins.then_inc(pe_turn_fold, 1)
                if exists(mid):
                    for k in (1, 2):
                        pe.wait_ge(act_in, DH * mid + k)
                        mlp_up(mid, k)
                    for k in (3, 4):
                        pe.wait_ge(act_gelu, HC * mid + k - 2)
                        mlp_up(mid, k)
                if exists(back):
                    pe.wait_ge(dve_fold_lo, back + 1)
                    for x in range(2):
                        ins = mm3(turn[0:NF, x, :], dft_h[:, x, 0:NF], dft_l[:, x, 0:NF], fold_h[:, x, :],
                                  fold_l[:, x, :], True, True)
                    ins.then_inc(pe_dft, 1)
                if exists(mid):
                    pe.wait_ge(act_gelu, HC * mid + 3)
                    mlp_up(mid, 5)
                if exists(tail):
                    for m in range(DH):
                        if exists(mid):
                            pe.wait_ge(act_gelu, HC * mid + 4 + m)
                        for c in range(DH):
                            if m == 1 and c == 0:
                                pe.wait_ge(gate_done, tail + 1)
                                for t in range(TILES):
                                    ins = pe.transpose(gate_ps[0:ROUTED, t * TT:(t + 1) * TT], gated[:, t, :],
                                                       ident[0:TT, 0:TT])
                                ins.then_inc(pe_turn_gated, 1)
                            mm3(big[FFN_BANK[m]][:, 0:GT], base_h[:, c, m * P:(m + 1) * P],
                                base_l[:, c, m * P:(m + 1) * P], x2_h[:, c, :], x2_l[:, c, :], c == 0, False)
                if exists(mid):
                    pe.wait_ge(act_gelu, HC * mid + 6)
                for m in range(DH):
                    if exists(mid):
                        mlp_up(mid, 6, (m,))
                    if exists(tail):
                        if m == 0:
                            pe.wait_ge(dve_gated_lo, tail + 1)
                        mm3(big[FFN_BANK[m]][:, 0:GT], routedb_h[:, m * P:(m + 1) * P],
                            routedb_l[:, m * P:(m + 1) * P], gated_h[:, :], gated_l[:, :], False, True)\
                            .then_inc(pe_ffn, 1)
                if exists(mid):
                    if exists(tail):
                        pe.wait_ge(dve_result, DH * tail + 1)
                    mlp_up(mid, 7)
                if exists(front):
                    if exists(tail):
                        pe.wait_ge(dve_result, DH * tail + 2)
                    elif exists(mid):
                        pe.wait_ge(act_gelu, HC * mid + 5)
                    else:
                        pe.wait_ge(weight_lo, 1)
                    embed(front, 0)
                if exists(back):
                    pe.wait_ge(dve_spec, 3 * back + 3)
                    for m in range(DH):
                        for img in range(PAIR):
                            c = img * DIM + m * P
                            ps = turn[:, m, img * N_TOK:(img + 1) * N_TOK]
                            pe.matmul(ps, spec_y[:, 0, c:c + P], cos_inv[:, :], start=True, stop=False)
                            ins = pe.matmul(ps, spec_y[:, 1, c:c + P], sin_inv[:, :], start=False, stop=True)
                    ins.then_inc(pe_idft, 1)
                if exists(front):
                    if exists(mid):
                        pe.wait_ge(act_gelu, HC * mid + 7)
                    embed(front, 1)
                if exists(back):
                    pe.wait_ge(dve_y_lo, back + 1)
                    for m in range(DH):
                        if m == 0:
                            if exists(mid):
                                pe.wait_ge(act_gelu, HC * mid + 8)
                            else:
                                pe.wait_ge(dve_result, DH * tail + 1)
                        elif exists(front):
                            pe.wait_ge(act_h, DH * front + 1)
                        else:
                            pe.wait_ge(dve_result, DH * tail + 2)
                        for c in range(DH):
                            ins = mm3(big[OUT_BANK[m]][:, 0:GT], outw_h[:, c, m * P:(m + 1) * P],
                                      outw_l[:, c, m * P:(m + 1) * P], y_h[:, c, :], y_l[:, c, :],
                                      c == 0, c == DH - 1)
                        ins.then_inc(pe_out, 1)
                if exists(front):
                    pe.wait_ge(act_h, DH * front + 2)
                    to_tokens(turn, h_sb[:, slot], pe_turn_h)
                if exists(back):
                    pe.wait_ge(dve_h2, DH * back + 2)
                    to_tokens(turn2, h_sb[:, (slot + 1) % SLOTS], pe_turn_h2)
                if exists(mid):
                    if not exists(mid - 1):
                        pe.wait_ge(weight_lo, 9)
                    mlp_down(mid, 0, range(8))
                    mlp_down(mid, 1, range(4))
                if exists(front):
                    pe.wait_ge(act_norm1, front + 1)
                    pe.wait_ge(dve_norm1, front + 1)
                    to_features(turn, norm1, pe_turn_x1)
                if exists(mid):
                    mlp_down(mid, 1, range(4, 8))
                if exists(back):
                    pe.wait_ge(act_norm2, back + 1)
                    pe.wait_ge(dve_norm2, back + 1)
                    to_features(turn2, norm2, pe_turn_x2)

            for i in range(3):
                step(i, i)
            with pe.Fori(3, LOOP_END, SLOTS) as i:
                for slot in range(SLOTS):
                    step(i + slot, slot)
            for i in range(GROUPS - 2, GROUPS + 3):
                step(i, i % SLOTS)


def shape_constants():
    f, t = np.arange(NF), np.arange(N_TOK)
    angle = 2 * np.pi * ((f[:, None] * t[None, :]) % N_TOK) / N_TOK
    cos, sin = np.cos(angle), np.sin(angle)
    sin[[0, HALF], :] = 0.0
    sin[:, [0, HALF]] = 0.0
    weight = np.where((f == 0) | (f == HALF), 1.0, 2.0) / N_TOK
    fwd = cos[:, :NF].copy()
    fwd[HALF] *= 0.5
    earlier = np.tril(np.ones((EXPERTS, EXPERTS)), -1) * -TINY
    c32 = lambda a: np.ascontiguousarray(a, dtype=np.float32)
    return {
        "ident": c32(np.eye(P)),
        "cos_fwd": c32(fwd),
        "sin_fwd": c32(-sin[:, :NF]),
        "cos_inv": c32(cos),
        "sin_inv": c32(-sin),
        "cos_tap": c32((weight[:, None] * cos[:, :TAPS]).T),
        "sin_tap": c32((weight[:, None] * -sin[:, :TAPS]).T),
        "rank_thr": c32(np.broadcast_to(earlier, (TT, TILES, EXPERTS, EXPERTS)).reshape(TT, -1)),
    }


def kernel(**inputs):
    import concourse.bacc as bacc
    from concourse.bass_utils import run_bass_kernel_spmd

    a = {k: np.asarray(v) for k, v in inputs.items()}
    x = a["x"].reshape(IMAGES, CHANNELS, GRID, PATCH, GRID, PATCH).transpose(0, 1, 3, 5, 2, 4)
    x = x.reshape(IMAGES, N_TOK, FLAT).reshape(GROUPS, GT, KT, P).transpose(0, 3, 2, 1)
    consts = shape_constants()
    pre = "L0_"
    columns = [a[pre + k].reshape(-1, P) for k in
               ("attn_in_b", "attn_mod_b2", "attn_out_b", "ffn_base_b", "attn_mod_b1")]
    route_column = np.zeros((1, P), np.float32)
    route_column[0, ROUTED:ROUTE_COLS] = a[pre + "ffn_router_b"]
    biases = np.concatenate([*columns, route_column]).T
    arrays = {
        "xg": x,
        "tok_w": a[pre + "tok_W"],
        "in_w": a[pre + "attn_in_w"],
        "w1": a[pre + "attn_mod_w1"],
        "w2": a[pre + "attn_mod_w2"],
        "taps_t": a[pre + "attn_kernel"].T,
        "out_w": a[pre + "attn_out_w"],
        "base_wt": a[pre + "ffn_base_W"].T,
        "shared_a": a[pre + "ffn_shared_A"],
        "shared_bt": a[pre + "ffn_shared_B"].T,
        "route_w": np.concatenate([a[pre + "ffn_routed_A"].reshape(ROUTED, DIM), a[pre + "ffn_router_W"]]).T,
        "routed_bt": a[pre + "ffn_routed_B"].transpose(0, 2, 1).reshape(ROUTED, DIM),
        "biases": biases,
        **consts,
    }
    arrays = {k: np.ascontiguousarray(v) for k, v in arrays.items()}
    nc = bacc.Bacc("TRN2", target_bir_lowering=False, num_devices=1)
    args = [nc.dram_tensor("dram_" + k, v.shape, mybir.dt.from_np(v.dtype), kind="ExternalInput").ap()
            for k, v in arrays.items()]
    out = nc.dram_tensor("out", (DIM, IMAGES * N_TOK), F32, kind="ExternalOutput").ap()
    tower_program(nc, *args, out)
    r = run_bass_kernel_spmd(nc, [{"dram_" + k: v for k, v in arrays.items()}], core_ids=[0])
    return np.ascontiguousarray(r.results[0]["out"].T).reshape(IMAGES, N_TOK, DIM)
```

```python
from contextlib import ExitStack

import numpy as np

import concourse.bass as bass
from concourse import mybir

F32 = mybir.dt.float32
F32R = mybir.dt.float32r
I32 = mybir.dt.int32
ACT = mybir.ActivationFunctionType
ALU = mybir.AluOpType
AX_X = mybir.AxisListType.X

P = 128
IMAGES, CHANNELS, SIDE, PATCH = 64, 3, 224, 16
GRID = SIDE // PATCH
N_TOK = GRID * GRID
FLAT = CHANNELS * PATCH * PATCH
DIM = 256
HID = 1024
TAPS = 64
EXPERTS, RANK = 6, 16
ROUTED = EXPERTS * RANK
ROUTE_COLS = ROUTED + EXPERTS
LN_EPS = 1e-5
GATE_EPS = 1e-6

PAIR = 2
GROUPS = IMAGES // PAIR
GT = PAIR * N_TOK
TILES = 4
TT = GT // TILES
KT = FLAT // P
DH = DIM // P
HC = HID // P
HALF = N_TOK // 2
NF = HALF + 1
NFP = NF + 1
INV = 128
SLOTS = 3
BANK = 512
CONSTS = 9
CHUNK = 2
RSQRT_MAGIC, RSQRT_K1, RSQRT_K2 = 1595932665.0, 0.703952253, 2.38924456
TINY = 1.1754944e-38
LOG2_E, ROUND, LEAST_EXP, EXP_BIAS, EXP_UNIT = 1.4426950408889634, 1.5 * 2.0 ** 23, -87.0, 127.0, 2.0 ** 23
EXP2_POLY = (0.0001546734499, 0.001340038947, 0.009618036033,
             0.05550327361, 0.2402265108, 0.6931472066)
LOOP_END = GROUPS - 2 - SLOTS + 1

EARLY_K, LATE_K = range(KT // 2), range(KT // 2, KT)
LN_STEPS = 16
GATE_STEPS = 24
EXP_STEPS = 13


def exists(g):
    return 0 <= g < GROUPS if isinstance(g, int) else True


def tower_program(nc: bass.Bass, xg, tok_w, in_w, w1, w2, taps_t, out_w, base_wt,
                  shared_a, shared_bt, route_w, routed_bt, biases_d, ident_d, cos_fwd_d, sin_fwd_d, cos_inv_d,
                  sin_inv_d, cos_tap_d, sin_tap_d, rank_thr_d, out):
    ctx = ExitStack()
    with ctx:
        def sb(name, shape, dt=F32):
            return ctx.enter_context(nc.sbuf_tensor(name, shape, dt))

        def sem(name):
            return ctx.enter_context(nc.semaphore(name))

        def pair(name, shape):
            return sb(name + "_h", shape, F32R), sb(name + "_l", shape, F32R)

        tokw_h, tokw_l = pair("tokw", [P, KT, DIM])
        inw_h, inw_l = pair("inw", [P, DH, DIM])
        w1_h, w1_l = pair("w1", [P, DH, HID])
        w2_h, w2_l = pair("w2", [P, HC, DIM])
        outw_h, outw_l = pair("outw", [P, DH, DIM])
        route_h, route_l = pair("route", [P, DH, ROUTE_COLS])
        base_h, base_l = pair("base", [P, DH, DIM])
        routedb_h, routedb_l = pair("routedb", [ROUTED, DIM])
        dft_h, dft_l = pair("dft", [NF, 2, 100])
        inverse = sb("inverse", [NF, 2, INV])
        spec_k = sb("spec_k", [NF, 2, PAIR * DIM])
        ident = sb("ident", [P, P])
        rank_thr = sb("rank_thr", [TT, TILES * EXPERTS * EXPERTS])
        biases = sb("biases", [P, 4 * DH + HC + 1])
        in_bias = biases[:, 0:DH]
        b2_bias = biases[:, DH:2 * DH]
        out_bias = biases[:, 2 * DH:3 * DH]
        base_bias = biases[:, 3 * DH:4 * DH]
        b1_bias = biases[:, 4 * DH:4 * DH + HC]
        route_bias = biases[0:ROUTE_COLS, 4 * DH + HC:4 * DH + HC + 1]

        patches = sb("patches", [P, KT, GT])
        patches_h, patches_l = pair("patches", [P, KT, GT])
        h_sb = sb("h_sb", [P, SLOTS, DH, GT])
        norm1 = sb("norm1", [TT, TILES, DIM])
        norm2 = sb("norm2", [TT, TILES, DIM])
        x1_h, x1_l = pair("x1", [P, DH, GT])
        x2_h, x2_l = pair("x2", [P, DH, GT])
        x_proj = sb("x_proj", [P, DH, GT])
        gelu = sb("gelu", [P, 4, GT])
        gelu_h, gelu_l = pair("gelu", [P, HC, GT])
        modulated = sb("modulated", [P, DH, PAIR, N_TOK])
        folded = sb("folded", [P, DH, 2, PAIR, NFP])
        fold_h, fold_l = pair("fold", [NF, 2, PAIR * DIM])
        prod = sb("prod", [P, 2, 2, PAIR * DIM])
        spec_y = sb("spec_y", [NF, 2, PAIR * DIM])
        y_sin = sb("y_sin", [P, DH, PAIR, NF])
        y = sb("y", [P, DH, PAIR, N_TOK])
        y_h, y_l = pair("y", [P, DH, GT])
        route_sb = sb("route_sb", [ROUTE_COLS, GT])
        gated = sb("gated", [TT, TILES, ROUTED])
        gated_h, gated_l = pair("gated", [ROUTED, GT])
        result = sb("result", [P, DH, GT])
        flat_y = y[:, :, :, :].rearrange("p m i t -> p (m i t)")
        shared_sb = flat_y[0:RANK, 0:2 * DIM]
        taps = flat_y[0:TAPS, 2 * DIM:3 * DIM]
        tap_mats = y_sin[0:TAPS, 0]
        bn = sb("bn", [TT, 2, TILES, 6])
        mean_var = sb("mean_var", [TT, 2, TILES, 2])
        ln_tmp = sb("ln_tmp", [TT, 15, 2, TILES])
        gate_small = sb("gate_small", [TT, 8, TILES])
        gate_wide = sb("gate_wide", [TT, 11, TILES, EXPERTS])
        gate_cmp = sb("gate_cmp", [TT, 2, TILES, EXPERTS, EXPERTS])

        big = [ctx.enter_context(nc.psum_tensor(f"big{n}", [P, BANK], F32)) for n in range(3)]
        turn = ctx.enter_context(nc.psum_tensor("turn", [P, 2, BANK], F32))
        turn2 = ctx.enter_context(nc.psum_tensor("turn2", [P, 2, BANK], F32))
        IN_BANK, UP_BANK, FFN_BANK = (0, 1), (2, 0, 1, 2, 0, 1, 1, 2), (2, 0)
        EMBED_BANK, OUT_BANK, DOWN_BANK = (0, 1), (2, 0), (1, 2)
        inverted = turn[:, :, :].rearrange("p m (i x t) -> p m i x t", i=PAIR, x=2)
        gate_ps = ctx.enter_context(nc.psum_tensor("gate_ps", [P, BANK], F32))

        tok_w_in = [sem(f"tok_w_in{n}") for n in range(KT // CHUNK)]
        first_in = [sem(f"first_in{n}") for n in range(KT // CHUNK)]
        weight_in = {n: sem(n + "_in") for n in ("in_w", "w1", "w2", "dft", "route", "out_w", "routedb", "base")}
        ident_in = sem("ident_in")
        const_in = sem("const_in")
        patches_in = sem("patches_in")
        result_out = sem("result_out")
        pad_zero = sem("pad_zero")
        tok_w_hi = sem("tok_w_hi")
        weight_hi = sem("weight_hi")
        tok_w_lo = sem("tok_w_lo")
        dve_weight_lo = sem("dve_weight_lo")
        pool_weight_lo = sem("pool_weight_lo")
        dve_first_lo = sem("dve_first_lo")
        setup_mm = sem("setup_mm")
        spectrum_ready = sem("spectrum_ready")
        base_sum = sem("base_sum")
        pe_embed = sem("pe_embed")
        pe_turn_h = sem("pe_turn_h")
        pe_turn_x1 = sem("pe_turn_x1")
        pe_in = sem("pe_in")
        pe_w1 = sem("pe_w1")
        pe_w2 = sem("pe_w2")
        pe_turn_fold = sem("pe_turn_fold")
        pe_dft = sem("pe_dft")
        pe_idft = sem("pe_idft")
        pe_out = sem("pe_out")
        pe_turn_h2 = sem("pe_turn_h2")
        pe_turn_x2 = sem("pe_turn_x2")
        pe_route = sem("pe_route")
        pe_turn_route = sem("pe_turn_route")
        pe_turn_gated = sem("pe_turn_gated")
        pe_ffn = sem("pe_ffn")
        act_patches_hi = sem("act_patches_hi")
        act_h = sem("act_h")
        act_norm1 = sem("act_norm1")
        act_x1_hi = sem("act_x1_hi")
        act_in = sem("act_in")
        act_gelu = sem("act_gelu")
        act_gelu_hi = sem("act_gelu_hi")
        act_fold_hi = sem("act_fold_hi")
        act_y_sin = sem("act_y_sin")
        act_y_hi = sem("act_y_hi")
        act_norm2 = sem("act_norm2")
        act_x2_hi = sem("act_x2_hi")
        act_route = sem("act_route")
        act_gated_hi = sem("act_gated_hi")
        dve_ln = sem("dve_ln")
        dve_norm1 = sem("dve_norm1")
        dve_norm2 = sem("dve_norm2")
        dve_x1_lo = sem("dve_x1_lo")
        dve_gelu_lo = sem("dve_gelu_lo")
        dve_mod = sem("dve_mod")
        dve_fold_lo = sem("dve_fold_lo")
        dve_spec = sem("dve_spec")
        dve_y = sem("dve_y")
        dve_y_lo = sem("dve_y_lo")
        dve_h2 = sem("dve_h2")
        dve_x2_lo = sem("dve_x2_lo")
        dve_gate = sem("dve_gate")
        gate_done = sem("gate_done")
        dve_gated_lo = sem("dve_gated_lo")
        dve_result = sem("dve_result")
        pool_patches_lo = sem("pool_patches_lo")
        pool_fold = sem("pool_fold")

        out_v = out.rearrange("(m p) t -> p m t", p=P)

        blocks = lambda w: w.rearrange("(k p) n -> p k n", p=P)
        flat_prod = prod[:, :, :, :].rearrange("p a b n -> p (a b n)")
        flat_modulated = modulated[:, :, :, :].rearrange("p m a t -> p (m a t)")
        flat_folded = folded[:, :, :, :, :].rearrange("p m x a t -> p (m x a t)")
        late_h = h_sb[:, 1:SLOTS].rearrange("p s m t -> p (s m t)")
        place = lambda a, start, k, n: a[:, start:start + k * n].rearrange("p (k n) -> p k n", k=k)
        tokw_wait = place(flat_prod, 0, KT, DIM)

        def pieces(src, w, places):
            k, out = 0, []
            for waiting in places:
                ks = slice(k, k + waiting.shape[1])
                out.append((blocks(src)[:, ks, :], waiting, w[0][:, ks, :], w[1][:, ks, :]))
                k = ks.stop
            return out

        splits = {
            "in_w": pieces(in_w, (inw_h, inw_l), [x_proj[:, :, 0:DIM]]),
            "w1": pieces(w1, (w1_h, w1_l), [place(gelu[:, :, :].rearrange("p k t -> p (k t)"), 0, 1, HID),
                                            place(late_h, 0, 1, HID)]),
            "w2": pieces(w2, (w2_h, w2_l), [place(flat_prod, KT * DIM, 2, DIM), place(late_h, HID, 2, DIM),
                                            place(result[:, :, :].rearrange("p m t -> p (m t)"), 0, 3, DIM),
                                            place(flat_folded, DH * DIM, 1, DIM)]),
            "dft": [(None, spec_y[:, :, 0:NF], dft_h[:, :, 0:NF], dft_l[:, :, 0:NF])],
            "route": pieces(route_w, (route_h, route_l), [place(flat_modulated, DH * DIM, DH, ROUTE_COLS)]),
            "out_w": pieces(out_w, (outw_h, outw_l), [place(flat_folded, 0, DH, DIM)]),
            "routedb": [(routed_bt, norm2[0:ROUTED, 0, :], routedb_h[:, :], routedb_l[:, :])],
            "base": pieces(base_wt, (base_h, base_l), [place(flat_modulated, 0, DH, DIM)]),
        }
        base_wait = splits["base"][0][1]
        ORDER = list(splits)
        DVE_SPLITS, POOL_SPLITS = ORDER[:2], ORDER[2:]

        block = ctx.enter_context(nc.Block())

        @block.sync
        def _(sp):
            def load_patches(g):
                sp.wait_ge(pool_patches_lo, KT * g + KT)
                sp.dma_start(patches[:, :, :], xg[bass.ds(g + 1, 1)].rearrange("g p k t -> p (g k) t"))\
                    .then_inc(patches_in, 16)

            def const(dst, src):
                sp.dma_start(dst, src).then_inc(const_in, 16)

            for n in range(KT // CHUNK):
                ks = slice(n * CHUNK, (n + 1) * CHUNK)
                sp.dma_start(patches[:, ks, :], xg[0][:, ks, :]).then_inc(first_in[n], 16)
            sp.dma_start(ident[:, :], ident_d).then_inc(ident_in, 16)

            def weight(n):
                for src, waiting, hi, lo in splits[n]:
                    sp.dma_start(waiting, src).then_inc(weight_in[n], 16)

            for n in ("in_w", "w1"):
                weight(n)
            const(taps[:, :], taps_t)
            const(tap_mats[:, 0, 0:NF], cos_tap_d)
            const(tap_mats[:, 1, 0:NF], sin_tap_d)
            const(shared_sb[:, 0:DIM], shared_a)
            const(shared_sb[:, DIM:2 * DIM], shared_bt)
            sp.wait_ge(dve_first_lo, KT // 2)
            load_patches(0)
            weight("w2")
            const(biases[:, :], biases_d)
            const(inverse[:, 0, :], cos_inv_d)
            const(inverse[:, 1, :], sin_inv_d)
            const(rank_thr[:, :], rank_thr_d)
            sp.dma_start(spec_y[:, 0, 0:NF], cos_fwd_d).then_inc(weight_in["dft"], 16)
            sp.dma_start(spec_y[:, 1, 0:NF], sin_fwd_d).then_inc(weight_in["dft"], 16)
            for n in ("route", "out_w", "routedb", "base"):
                weight(n)

            def step(i):
                front, tail = i, i - 3
                if exists(tail):
                    sp.wait_ge(dve_result, 2 * tail + 2)
                    sp.dma_start(out_v[:, :, bass.ds(tail * GT, GT)], result[:, :, :]).then_inc(result_out, 16)
                if exists(front + 1) and not (isinstance(i, int) and i == 0):
                    load_patches(front)

            for i in range(3):
                step(i)
            with sp.Fori(3, LOOP_END, SLOTS) as i:
                for slot in range(SLOTS):
                    step(i + slot)
            for i in range(GROUPS - 2, GROUPS + 3):
                step(i)
            sp.wait_ge(result_out, 16 * GROUPS)

        @block.gpsimd
        def _(pool):
            def patches_lo(g, ks):
                for k in ks:
                    pool.wait_ge(act_patches_hi, KT * g + k + 1)
                    pool.tensor_tensor(patches_l[:, k, :], patches[:, k, :], patches_h[:, k, :].bitcast(F32),
                                       ALU.subtract).then_inc(pool_patches_lo, 1)

            def weight_lo(n):
                pool.wait_ge(weight_hi, ORDER.index(n) + 1)
                for src, waiting, hi, lo in splits[n]:
                    ins = pool.tensor_tensor(lo, waiting, hi.bitcast(F32), ALU.subtract)
                ins.then_inc(pool_weight_lo, 1)

            for k in range(0, KT, 2):
                pool.wait_ge(act_patches_hi, k + 1)
                pool.tensor_tensor(patches_l[:, k, :], patches[:, k, :], patches_h[:, k, :].bitcast(F32),
                                   ALU.subtract).then_inc(pool_patches_lo, 2)

            def fold(g):
                for m in range(DH):
                    pool.wait_ge(dve_mod, DH * g + m + 1)
                    if m == 0:
                        if exists(g - 1):
                            pool.wait_ge(pe_turn_fold, g)
                        else:
                            pool.wait_ge(pad_zero, 1)
                    fwd = modulated[:, m, :, 1:NF]
                    back = modulated[:, m, :, N_TOK - 1:N_TOK - NF:-1]
                    pool.tensor_tensor(folded[:, m, 0, :, 1:NF], fwd, back, ALU.add)
                    pool.tensor_copy(folded[:, m, 0, :, 0:1], modulated[:, m, :, 0:1])
                    pool.tensor_tensor(folded[:, m, 1, :, 1:NF], fwd, back, ALU.subtract).then_inc(pool_fold, 1)

            def step(i):
                front, mid = i, i - 1
                if isinstance(i, int) and i == 0:
                    patches_lo(1, range(KT))
                    for n in POOL_SPLITS:
                        weight_lo(n)
                    pool.wait_ge(pool_weight_lo, len(POOL_SPLITS))
                    pool.memset(folded[:, :, :, :, :], 0.0).then_inc(pad_zero, 1)
                elif isinstance(i, int) and i == 1:
                    fold(mid)
                    patches_lo(front + 1, EARLY_K)
                else:
                    if exists(front):
                        patches_lo(front, LATE_K)
                    if exists(front + 1):
                        patches_lo(front + 1, EARLY_K)
                    if exists(mid):
                        fold(mid)

            for i in range(3):
                step(i)
            with pool.Fori(3, LOOP_END, SLOTS) as i:
                for slot in range(SLOTS):
                    step(i + slot)
            for i in range(GROUPS - 2, GROUPS + 3):
                step(i)

        @block.scalar
        def _(act):
            def weight_hi_part(n):
                act.wait_ge(weight_in[n], 32 if n == "dft" else 16 * len(splits[n]))
                if n == "base":
                    act.wait_ge(base_sum, DH)
                for src, waiting, hi, lo in splits[n]:
                    ins = act.activation(hi, waiting, ACT.Copy)
                ins.then_inc(weight_hi, 1)

            def patches_hi(g, ks):
                for k in ks:
                    if k == 0:
                        act.wait_ge(patches_in, 16 * g)
                        act.wait_ge(pe_embed, DH * g)
                    act.activation(patches_h[:, k, :], patches[:, k, :], ACT.Copy).then_inc(act_patches_hi, 1)

            for n in range(KT // CHUNK):
                ks = slice(n * CHUNK, (n + 1) * CHUNK)
                act.dma_start(tokw_wait[:, ks, :], blocks(tok_w)[:, ks, :]).then_inc(tok_w_in[n], 16)
            for n in range(KT // CHUNK):
                ks = slice(n * CHUNK, (n + 1) * CHUNK)
                act.wait_ge(tok_w_in[n], 16)
                act.activation(tokw_h[:, ks, :], tokw_wait[:, ks, :], ACT.Copy).then_inc(tok_w_hi, 1)
                act.wait_ge(first_in[n], 16)
                for k in range(n * CHUNK, (n + 1) * CHUNK):
                    act.activation(patches_h[:, k, :], patches[:, k, :], ACT.Copy).then_inc(act_patches_hi, 1)
            weight_hi_part("in_w")
            weight_hi_part("w1")

            def normalise(norm, which, ps, signal):
                for t in range(TILES // 2):
                    ins = act.activation(norm[:, t, :], ps[0:TT, 0, DIM * t:DIM * t + DIM], ACT.Identity,
                                         bias=ln_tmp[:, 1, which, t:t + 1], scale=ln_tmp[:, 0, which, t:t + 1])
                ins.then_inc(signal, 1)

            def project(g):
                for m in range(DH):
                    act.wait_ge(pe_in, DH * g + m + 1)
                    if m == 0:
                        if exists(g - 1):
                            act.wait_ge(dve_mod, DH * g)
                        else:
                            act.wait_ge(const_in, 16 * CONSTS)
                    act.activation(x_proj[:, m, :], big[IN_BANK[m]][:, 0:GT], ACT.Identity,
                                   bias=in_bias[:, m:m + 1]).then_inc(act_in, 1)

            def embedded(g, slot, m):
                act.wait_ge(pe_embed, DH * g + m + 1)
                act.activation(h_sb[:, slot, m, :], big[EMBED_BANK[m]][:, 0:GT], ACT.Copy).then_inc(act_h, 1)

            def gelu_tile(g, k):
                act.wait_ge(pe_w1, HC * g + k + 1)
                if k % 2 == 0:
                    if k >= 4:
                        act.wait_ge(dve_gelu_lo, 4 * g + k // 2 - 1)
                    elif exists(g - 1):
                        act.wait_ge(dve_gelu_lo, 4 * (g - 1) + k // 2 + 3)
                act.activation(gelu[:, k % 4, :], big[UP_BANK[k]][:, 0:GT], ACT.Gelu,
                               bias=b1_bias[:, k:k + 1]).then_inc(act_gelu, 1)

            def gelu_hi(g, j):
                act.wait_ge(act_gelu, HC * g + 2 * j + 2)
                s = (2 * j) % 4
                act.activation(gelu_h[:, 2 * j:2 * j + 2, :], gelu[:, s:s + 2, :], ACT.Copy)\
                    .then_inc(act_gelu_hi, 1)

            def fold_hi(g):
                act.wait_ge(pe_turn_fold, g + 1)
                act.activation(fold_h[:, :, :], turn[0:NF, :, :], ACT.Copy).then_inc(act_fold_hi, 1)

            def y_hi(g):
                for m in range(DH):
                    act.wait_ge(pe_idft, DH * g + m + 1)
                    if m == 0 and exists(g - 1):
                        act.wait_ge(dve_y, DH * g)
                    act.activation(y_sin[:, m], inverted[:, m, :, 1, 0:NF], ACT.Copy).then_inc(act_y_sin, 1)
                for m in range(DH):
                    act.wait_ge(dve_y, DH * g + m + 1)
                    act.activation(y_h[:, m, :], y[:, m].rearrange("p i t -> p (i t)"), ACT.Copy)\
                        .then_inc(act_y_hi, 1)

            def x2_hi(g):
                for m in range(DH):
                    act.wait_ge(pe_turn_x2, DH * g + m + 1)
                    act.activation(x2_h[:, m, :], turn2[:, m, 0:GT], ACT.Copy).then_inc(act_x2_hi, 1)

            def route(g):
                act.wait_ge(pe_route, g + 1)
                act.activation(route_sb[:, :], gate_ps[0:ROUTE_COLS, 0:GT], ACT.Identity,
                               bias=route_bias).then_inc(act_route, 1)

            def gated_hi(g):
                act.wait_ge(pe_turn_gated, g + 1)
                act.activation(gated_h[:, :], gate_ps[0:ROUTED, 0:GT], ACT.Copy).then_inc(act_gated_hi, 1)

            def step(i, slot):
                front, mid, back, tail = i, i - 1, i - 2, i - 3
                first, second = isinstance(i, int) and i == 0, isinstance(i, int) and i == 1
                if exists(mid):
                    project(mid)
                if exists(tail):
                    route(tail)
                if exists(mid):
                    gelu_tile(mid, 0)
                if exists(back):
                    fold_hi(back)
                if exists(mid):
                    gelu_tile(mid, 1)
                    gelu_hi(mid, 0)
                    gelu_tile(mid, 2)
                    gelu_tile(mid, 3)
                    gelu_hi(mid, 1)
                    gelu_tile(mid, 4)
                    gelu_tile(mid, 5)
                if exists(tail):
                    gated_hi(tail)
                if exists(mid):
                    gelu_hi(mid, 2)
                if exists(front) and not first and not second:
                    patches_hi(front, LATE_K)
                if exists(mid):
                    gelu_tile(mid, 6)
                    gelu_tile(mid, 7)
                    gelu_hi(mid, 3)
                if second:
                    for n in POOL_SPLITS[1:]:
                        weight_hi_part(n)
                if exists(back):
                    y_hi(back)
                if exists(front) and not second:
                    if exists(tail):
                        act.wait_ge(dve_result, DH * tail + 2)
                    elif exists(mid):
                        act.wait_ge(pool_weight_lo, POOL_SPLITS.index("w2") + 1)
                    for m in range(DH):
                        embedded(front, slot, m)
                if first:
                    patches_hi(1, range(KT))
                act.wait_ge(dve_ln, LN_STEPS * i + LN_STEPS)
                if exists(front):
                    normalise(norm1, 0, turn, act_norm1)
                if exists(back):
                    normalise(norm2, 1, turn2, act_norm2)
                if first:
                    act.wait_ge(dve_weight_lo, len(DVE_SPLITS))
                    embedded(1, 1, 0)
                if exists(front):
                    act.wait_ge(pe_turn_x1, DH * front + DH)
                    act.activation(x1_h[:, :, :], turn[:, :, 0:GT], ACT.Copy).then_inc(act_x1_hi, 1)
                if first:
                    weight_hi_part("w2")
                    embedded(1, 1, 1)
                elif exists(front + 1):
                    patches_hi(front + 1, EARLY_K)
                if exists(back):
                    x2_hi(back)

            def drain():
                mid, back, tail = GROUPS - 1, GROUPS - 2, GROUPS - 3
                project(mid)
                route(tail)
                gelu_tile(mid, 0)
                fold_hi(back)
                gelu_tile(mid, 1)
                gelu_hi(mid, 0)
                gelu_tile(mid, 2)
                gelu_tile(mid, 3)
                gelu_hi(mid, 1)
                gelu_tile(mid, 4)
                gelu_tile(mid, 5)
                gated_hi(tail)
                gelu_hi(mid, 2)
                gelu_tile(mid, 6)
                gelu_tile(mid, 7)
                gelu_hi(mid, 3)
                y_hi(back)
                fold_hi(mid)
                act.wait_ge(dve_ln, LN_STEPS * (GROUPS + 1))
                normalise(norm2, 1, turn2, act_norm2)
                x2_hi(back)
                back, tail = GROUPS - 1, GROUPS - 2
                route(tail)
                y_hi(back)
                gated_hi(tail)
                act.wait_ge(dve_ln, LN_STEPS * (GROUPS + 2))
                normalise(norm2, 1, turn2, act_norm2)
                x2_hi(back)
                route(back)
                gated_hi(back)

            for i in range(3):
                step(i, i)
            with act.Fori(3, LOOP_END, SLOTS) as i:
                for slot in range(SLOTS):
                    step(i + slot, slot)
            for i in range(GROUPS - 2, GROUPS):
                step(i, i % SLOTS)
            drain()

        @block.vector
        def _(dve):
            def weight_lo(n):
                dve.wait_ge(weight_hi, ORDER.index(n) + 1)
                for src, waiting, hi, lo in splits[n]:
                    ins = dve.tensor_tensor(lo, waiting, hi.bitcast(F32), ALU.subtract)
                ins.then_inc(dve_weight_lo, 1)

            for n in range(KT // CHUNK):
                ks = slice(n * CHUNK, (n + 1) * CHUNK)
                dve.wait_ge(tok_w_hi, n + 1)
                dve.tensor_tensor(tokw_l[:, ks, :], tokw_wait[:, ks, :], tokw_h[:, ks, :].bitcast(F32),
                                  ALU.subtract).then_inc(tok_w_lo, 1)
                for k in range(n * CHUNK + 1, (n + 1) * CHUNK, 2):
                    dve.wait_ge(act_patches_hi, k + 1)
                    dve.tensor_tensor(patches_l[:, k, :], patches[:, k, :], patches_h[:, k, :].bitcast(F32),
                                      ALU.subtract).then_inc(dve_first_lo, 1)
            for n in DVE_SPLITS:
                weight_lo(n)

            def setup_sums():
                dve.wait_ge(setup_mm, 2 + DH)
                for img in range(PAIR):
                    ins = dve.tensor_copy(spec_k[:, :, img * DIM:(img + 1) * DIM], turn2[0:NF, :, 0:DIM])
                ins.then_inc(spectrum_ready, 1)
                dve.wait_ge(weight_in["base"], 16)
                for k in range(DH):
                    dve.tensor_tensor(base_wait[:, k, :], turn2[:, k, DIM:2 * DIM], base_wait[:, k, :], ALU.add)\
                        .then_inc(base_sum, 1)

            def bn_stats(g, which, ps, ready):
                for t in range(TILES):
                    if t % 2 == 0:
                        dve.wait_ge(ready, 2 * g + t // 2 + 1)
                    ins = dve.bn_stats(bn[:, which, t, :], ps[0:TT, t // 2, DIM * (t % 2):DIM * (t % 2) + DIM])
                return ins

            def layer_norm_scales(i, stats, norms):
                done = [0]
                tmp = lambda n: ln_tmp[:, n, norms, :]

                def link(ins, wait=True):
                    done[0] += 1
                    ins.then_inc(dve_ln, 1)
                    if wait:
                        dve.wait_ge(dve_ln, LN_STEPS * i + done[0])

                link(stats)
                mean_m2 = mean_var[:, norms]
                link(dve.tensor_reduce(mean_m2, bn[:, norms].rearrange("p w t (x f) -> p w t f x", x=2)
                                       [:, :, :, 1:3, :], AX_X, ALU.add), wait=False)
                diff, within, between = tmp(12), tmp(13), tmp(14)
                link(dve.tensor_tensor(diff, bn[:, norms, :, 1], bn[:, norms, :, 4], ALU.subtract))
                link(dve.tensor_scalar(within, mean_m2[:, :, :, 1], 1.0 / DIM, LN_EPS, ALU.mult, ALU.add),
                     wait=False)
                link(dve.scalar_tensor_tensor(out=between, in0=diff, scalar=0.25, in1=diff, op0=ALU.mult,
                                              op1=ALU.mult))
                v = tmp(2)
                link(dve.tensor_tensor(v, within, between, ALU.add))
                guess, r1, r = tmp(3), tmp(6), tmp(0)
                link(dve.tensor_scalar(guess.bitcast(I32), v.bitcast(I32), -0.5, RSQRT_MAGIC, ALU.mult, ALU.add))
                link(dve.tensor_tensor(tmp(4), guess, guess, ALU.mult))
                link(dve.scalar_tensor_tensor(out=tmp(5), in0=tmp(4), scalar=-RSQRT_K1, in1=v, op0=ALU.mult,
                                              op1=ALU.mult))
                link(dve.scalar_tensor_tensor(out=r1, in0=tmp(5), scalar=RSQRT_K1 * RSQRT_K2, in1=guess,
                                              op0=ALU.add, op1=ALU.mult))
                link(dve.tensor_scalar(tmp(7), r1, 0.375, None, ALU.mult), wait=False)
                link(dve.tensor_tensor(tmp(8), r1, r1, ALU.mult))
                link(dve.tensor_tensor(tmp(9), tmp(8), v, ALU.mult))
                link(dve.scalar_tensor_tensor(out=tmp(10), in0=tmp(9), scalar=-10.0 / 3.0, in1=tmp(9),
                                              op0=ALU.add, op1=ALU.mult))
                link(dve.scalar_tensor_tensor(out=r, in0=tmp(10), scalar=5.0, in1=tmp(7), op0=ALU.add,
                                              op1=ALU.mult))
                link(dve.scalar_tensor_tensor(out=tmp(1), in0=mean_m2[:, :, :, 0], scalar=-0.5, in1=r,
                                              op0=ALU.mult, op1=ALU.mult))
                assert done[0] == LN_STEPS

            def normalise(norm, which, ps, signal):
                for t in range(TILES // 2, TILES):
                    c = DIM * (t - TILES // 2)
                    ins = dve.tensor_scalar(norm[:, t, :], ps[0:TT, 1, c:c + DIM], ln_tmp[:, 0, which, t:t + 1],
                                            ln_tmp[:, 1, which, t:t + 1], ALU.mult, ALU.add)
                ins.then_inc(signal, 1)

            def over_experts(a):
                return a.rearrange("p (t a) -> p t a", a=1).broadcast_to([TT, TILES, EXPERTS])

            rows = gate_ps[0:TT, 0:TILES * ROUTE_COLS].rearrange("p (t c) -> p t c", t=TILES)
            small = lambda n: gate_small[:, n, :]
            wide = lambda n: gate_wide[:, n].rearrange("p t e -> p (t e)")

            def gate_exp(g):
                done = [0]

                def link(ins, wait=True):
                    done[0] += 1
                    ins.then_inc(dve_gate, 1)
                    if wait:
                        dve.wait_ge(dve_gate, GATE_STEPS * g + done[0])

                logits = rows[:, :, ROUTED:ROUTE_COLS]
                dve.wait_ge(pe_turn_route, g + 1)
                link(dve.tensor_reduce(small(0), logits, AX_X, ALU.max))
                link(dve.tensor_tensor(gate_wide[:, 0], logits, over_experts(small(0)), ALU.subtract))
                scaled, whole, part, power, poly = (wide(n) for n in range(6, 11))
                link(dve.tensor_scalar(scaled, wide(0), LEAST_EXP, LOG2_E, ALU.max, ALU.mult))
                link(dve.tensor_scalar(whole, scaled, ROUND, ROUND, ALU.add, ALU.subtract))
                link(dve.tensor_tensor(part, scaled, whole, ALU.subtract), wait=False)
                link(dve.tensor_scalar(power.bitcast(I32), whole, EXP_BIAS, EXP_UNIT, ALU.add, ALU.mult))
                link(dve.tensor_scalar(poly, part, EXP2_POLY[0], None, ALU.mult))
                for coef in EXP2_POLY[1:]:
                    link(dve.scalar_tensor_tensor(out=poly, in0=poly, scalar=coef, in1=part, op0=ALU.add,
                                                  op1=ALU.mult))
                link(dve.scalar_tensor_tensor(out=wide(1), in0=poly, scalar=1.0, in1=power, op0=ALU.add,
                                              op1=ALU.mult), wait=False)
                assert done[0] == EXP_STEPS

            def gate(g):
                done = [EXP_STEPS]

                def link(ins):
                    done[0] += 1
                    ins.then_inc(dve_gate, 1)
                    dve.wait_ge(dve_gate, GATE_STEPS * g + done[0])

                dve.wait_ge(dve_gate, GATE_STEPS * g + EXP_STEPS)
                link(dve.tensor_reduce(small(1), gate_wide[:, 1], AX_X, ALU.add))
                link(dve.reciprocal(small(2), small(1)))
                gates = gate_wide[:, 2]
                link(dve.tensor_tensor(gates, gate_wide[:, 1], over_experts(small(2)), ALU.mult))
                e4 = [TT, TILES, EXPERTS, EXPERTS]
                other = gates.rearrange("p t (a e) -> p t a e", a=1).broadcast_to(e4)
                own = gates.rearrange("p t (e a) -> p t e a", a=1).broadcast_to(e4)
                link(dve.tensor_tensor(gate_cmp[:, 0], other, own, ALU.subtract))
                flat = lambda n: gate_cmp[:, n].rearrange("p t e f -> p (t e f)")
                link(dve.tensor_tensor(flat(1), flat(0), rank_thr[:, :], ALU.is_gt))
                link(dve.tensor_reduce(gate_wide[:, 3], gate_cmp[:, 1], AX_X, ALU.add))
                link(dve.scalar_tensor_tensor(out=wide(4), in0=wide(3), scalar=1.5, in1=wide(2), op0=ALU.is_lt,
                                              op1=ALU.mult))
                link(dve.tensor_reduce(small(3), gate_wide[:, 4], AX_X, ALU.add))
                link(dve.tensor_scalar(small(4), small(3), GATE_EPS, None, ALU.add))
                link(dve.reciprocal(small(5), small(4)))
                link(dve.tensor_tensor(gate_wide[:, 5], gate_wide[:, 4], over_experts(small(5)), ALU.mult))
                assert done[0] == GATE_STEPS
                hidden = rows[:, :, 0:ROUTED].rearrange("p t (e r) -> p t e r", r=RANK)
                weight = gate_wide[:, 5].rearrange("p t (e a) -> p t e a", a=1)\
                    .broadcast_to([TT, TILES, EXPERTS, RANK])
                dve.tensor_tensor(gated[:, :, :].rearrange("p t (e r) -> p t e r", r=RANK), hidden, weight,
                                  ALU.mult).then_inc(gate_done, 1)

            def gelu_lo(g, j):
                dve.wait_ge(act_gelu_hi, 4 * g + j + 1)
                s = (2 * j) % 4
                dve.tensor_tensor(gelu_l[:, 2 * j:2 * j + 2, :], gelu[:, s:s + 2, :],
                                  gelu_h[:, 2 * j:2 * j + 2, :].bitcast(F32), ALU.subtract).then_inc(dve_gelu_lo, 1)

            def modulate(g, m):
                dve.wait_ge(pe_w2, DH * g + m + 1)
                dve.wait_ge(act_in, DH * g + m + 1)
                if exists(g - 1):
                    dve.wait_ge(pool_fold, DH * (g - 1) + m + 1)
                elif m == 0:
                    dve.wait_ge(const_in, 16 * CONSTS)
                    dve.wait_ge(pool_weight_lo, len(POOL_SPLITS))
                dve.scalar_tensor_tensor(out=modulated[:, m, :, :].rearrange("p a t -> p (a t)"),
                                         in0=big[DOWN_BANK[m]][:, 0:GT], scalar=b2_bias[:, m:m + 1],
                                         in1=x_proj[:, m, :], op0=ALU.add, op1=ALU.mult).then_inc(dve_mod, 1)

            def fold_lo(g):
                dve.wait_ge(act_fold_hi, g + 1)
                dve.tensor_tensor(fold_l[:, :, :], turn[0:NF, :, :], fold_h[:, :, :].bitcast(F32),
                                  ALU.subtract).then_inc(dve_fold_lo, 1)

            def products_with_spectrum(g, c):
                if c == 0:
                    dve.wait_ge(pe_dft, g + 1)
                    if not exists(g - 1):
                        dve.wait_ge(spectrum_ready, 1)
                for x in range(2):
                    ins = dve.tensor_tensor(prod[0:NF, c, x, :], turn[0:NF, x, :], spec_k[:, c, :], ALU.mult)
                if c == 1:
                    ins.then_inc(dve_spec, 1)

            def spectrum_of_y(g):
                dve.wait_ge(dve_spec, 3 * g + 1)
                dve.tensor_tensor(spec_y[:, 0, :], prod[0:NF, 0, 0, :], prod[0:NF, 1, 1, :], ALU.subtract)\
                    .then_inc(dve_spec, 1)
                dve.tensor_tensor(spec_y[:, 1, :], prod[0:NF, 0, 1, :], prod[0:NF, 1, 0, :], ALU.add)\
                    .then_inc(dve_spec, 1)

            def y_lo(g):
                for m in range(DH):
                    dve.wait_ge(act_y_sin, DH * g + m + 1)
                    dve.tensor_tensor(y[:, m, :, 0:NF], inverted[:, m, :, 0, 0:NF], y_sin[:, m], ALU.add)
                    dve.tensor_tensor(y[:, m, :, NF:N_TOK], inverted[:, m, :, 0, HALF - 1:0:-1],
                                      y_sin[:, m, :, HALF - 1:0:-1], ALU.subtract).then_inc(dve_y, 1)
                for m in range(DH):
                    dve.wait_ge(act_y_hi, DH * g + m + 1)
                    dve.tensor_tensor(y_l[:, m, :], y[:, m].rearrange("p i t -> p (i t)"),
                                      y_h[:, m, :].bitcast(F32), ALU.subtract).then_inc(dve_y_lo, 1)

            def add_mixer(g, slot):
                for m in range(DH):
                    dve.wait_ge(pe_out, DH * g + m + 1)
                    dve.scalar_tensor_tensor(out=h_sb[:, slot, m, :], in0=big[OUT_BANK[m]][:, 0:GT],
                                             scalar=out_bias[:, m:m + 1], in1=h_sb[:, slot, m, :],
                                             op0=ALU.add, op1=ALU.add).then_inc(dve_h2, 1)

            def x2_lo(g):
                for m in range(DH):
                    dve.wait_ge(act_x2_hi, DH * g + m + 1)
                    dve.tensor_tensor(x2_l[:, m, :], turn2[:, m, 0:GT], x2_h[:, m, :].bitcast(F32),
                                      ALU.subtract).then_inc(dve_x2_lo, 1)

            def gated_lo(g):
                dve.wait_ge(act_gated_hi, g + 1)
                dve.tensor_tensor(gated_l[:, :], gate_ps[0:ROUTED, 0:GT], gated_h[:, :].bitcast(F32),
                                  ALU.subtract).then_inc(dve_gated_lo, 1)

            def finish(g, slot):
                for m in range(DH):
                    dve.wait_ge(pe_ffn, DH * g + m + 1)
                    if m == 0 and exists(g - 1):
                        dve.wait_ge(result_out, 16 * g)
                    dve.scalar_tensor_tensor(out=result[:, m, :], in0=big[FFN_BANK[m]][:, 0:GT],
                                             scalar=base_bias[:, m:m + 1], in1=h_sb[:, slot, m, :], op0=ALU.add,
                                             op1=ALU.add).then_inc(dve_result, 1)

            def step(i, slot):
                front, mid, back, tail = i, i - 1, i - 2, i - 3
                if exists(tail):
                    gate_exp(tail)
                if exists(back):
                    fold_lo(back)
                if exists(mid):
                    gelu_lo(mid, 0)
                if exists(tail):
                    gate(tail)
                if exists(mid):
                    gelu_lo(mid, 1)
                if exists(tail):
                    gated_lo(tail)
                if exists(back):
                    products_with_spectrum(back, 0)
                if exists(tail):
                    finish(tail, slot)
                if exists(back):
                    products_with_spectrum(back, 1)
                    spectrum_of_y(back)
                if exists(mid):
                    gelu_lo(mid, 2)
                    gelu_lo(mid, 3)
                if exists(back):
                    y_lo(back)
                    add_mixer(back, (slot + 1) % SLOTS)
                stats = bn_stats(front, 0, turn, pe_turn_h)
                if exists(back):
                    stats = bn_stats(back, 1, turn2, pe_turn_h2)
                layer_norm_scales(i, stats, slice(0, 2 if exists(back) else 1))
                normalise(norm1, 0, turn, dve_norm1)
                if exists(back):
                    normalise(norm2, 1, turn2, dve_norm2)
                dve.wait_ge(act_x1_hi, front + 1)
                dve.tensor_tensor(x1_l[:, :, :], turn[:, :, 0:GT], x1_h[:, :, :].bitcast(F32), ALU.subtract)\
                    .then_inc(dve_x1_lo, 1)
                if isinstance(i, int) and i == 0:
                    setup_sums()
                if exists(mid):
                    modulate(mid, 0)
                    modulate(mid, 1)
                if exists(back):
                    x2_lo(back)

            def drain():
                mid, back, tail = GROUPS - 1, GROUPS - 2, GROUPS - 3
                gate_exp(tail)
                fold_lo(back)
                gelu_lo(mid, 0)
                gate(tail)
                gelu_lo(mid, 1)
                gated_lo(tail)
                products_with_spectrum(back, 0)
                finish(tail, tail % SLOTS)
                products_with_spectrum(back, 1)
                spectrum_of_y(back)
                gelu_lo(mid, 2)
                gelu_lo(mid, 3)
                y_lo(back)
                modulate(mid, 0)
                add_mixer(back, back % SLOTS)
                stats = bn_stats(back, 1, turn2, pe_turn_h2)
                modulate(mid, 1)
                layer_norm_scales(GROUPS, stats, slice(1, 2))
                normalise(norm2, 1, turn2, dve_norm2)
                fold_lo(mid)
                x2_lo(back)
                back, tail = GROUPS - 1, GROUPS - 2
                products_with_spectrum(back, 0)
                products_with_spectrum(back, 1)
                spectrum_of_y(back)
                gate_exp(tail)
                y_lo(back)
                gate(tail)
                add_mixer(back, back % SLOTS)
                stats = bn_stats(back, 1, turn2, pe_turn_h2)
                layer_norm_scales(GROUPS + 1, stats, slice(1, 2))
                normalise(norm2, 1, turn2, dve_norm2)
                gated_lo(tail)
                x2_lo(back)
                gate_exp(back)
                finish(tail, tail % SLOTS)
                gate(back)
                gated_lo(back)
                finish(back, back % SLOTS)

            for i in range(3):
                step(i, i)
            with dve.Fori(3, LOOP_END, SLOTS) as i:
                for slot in range(SLOTS):
                    step(i + slot, slot)
            for i in range(GROUPS - 2, GROUPS):
                step(i, i % SLOTS)
            drain()

        @block.tensor
        def _(pe):
            def mm3(ps, w_h, w_l, x_h, x_l, first, last):
                pe.matmul(ps, w_h, x_h, start=first, stop=False)
                pe.matmul(ps, w_h, x_l, start=False, stop=False)
                return pe.matmul(ps, w_l, x_h, start=False, stop=last)

            def embed_block(m, k):
                return mm3(big[EMBED_BANK[m]][:, 0:GT], tokw_h[:, k, m * P:(m + 1) * P],
                           tokw_l[:, k, m * P:(m + 1) * P], patches_h[:, k, :], patches_l[:, k, :],
                           k == 0, k == KT - 1)

            def embed(g, m):
                for k in range(KT):
                    if m == 0:
                        pe.wait_ge(pool_patches_lo, KT * g + k + 1)
                    ins = embed_block(m, k)
                ins.then_inc(pe_embed, 1)

            def embed_first():
                for k in range(KT):
                    pe.wait_ge(tok_w_lo, k // CHUNK + 1)
                    if k % 2 == 0:
                        pe.wait_ge(pool_patches_lo, k + 2)
                    else:
                        pe.wait_ge(dve_first_lo, k // 2 + 1)
                    for m in range(DH):
                        ins = embed_block(m, k)
                        if k == KT - 1:
                            ins.then_inc(pe_embed, 1)

            def to_tokens(ps, rows, signal):
                for t in range(TILES):
                    for m in range(DH):
                        c = DIM * (t % 2) + m * P
                        ins = pe.transpose(ps[0:TT, t // 2, c:c + P], rows[:, m, t * TT:(t + 1) * TT], ident[:, :])
                    if t % 2 == 1:
                        ins.then_inc(signal, 1)

            def to_features(ps, rows, signal):
                for m in range(DH):
                    for t in range(TILES):
                        ins = pe.transpose(ps[:, m, t * TT:(t + 1) * TT], rows[:, t, m * P:(m + 1) * P],
                                           ident[0:TT, 0:TT])
                    ins.then_inc(signal, 1)

            def mlp_up(g, k, cs=range(DH)):
                for c in cs:
                    ins = mm3(big[UP_BANK[k]][:, 0:GT], w1_h[:, c, k * P:(k + 1) * P],
                              w1_l[:, c, k * P:(k + 1) * P], x1_h[:, c, :], x1_l[:, c, :], c == 0, c == DH - 1)
                if cs[-1] == DH - 1:
                    ins.then_inc(pe_w1, 1)

            def mlp_down(g, m, cs):
                for c in cs:
                    if m == 0 and c % 2 == 0:
                        pe.wait_ge(dve_gelu_lo, 4 * g + c // 2 + 1)
                    ins = mm3(big[DOWN_BANK[m]][:, 0:GT], w2_h[:, c, m * P:(m + 1) * P],
                              w2_l[:, c, m * P:(m + 1) * P], gelu_h[:, c, :], gelu_l[:, c, :],
                              c == 0, c == HC - 1)
                if cs[-1] == HC - 1:
                    ins.then_inc(pe_w2, 1)

            def setup_products():
                pe.wait_ge(const_in, 16 * CONSTS)
                for c in range(2):
                    pe.matmul(turn2[0:NF, c, 0:DIM], tap_mats[:, c, 0:NF], taps[:, :], start=True, stop=True)\
                        .then_inc(setup_mm, 1)
                for k in range(DH):
                    pe.matmul(turn2[:, k, DIM:2 * DIM], shared_sb[:, k * P:(k + 1) * P],
                              shared_sb[:, DIM:2 * DIM], start=True, stop=True).then_inc(setup_mm, 1)

            def route(g):
                for c in range(DH):
                    pe.wait_ge(dve_x2_lo, DH * g + c + 1)
                    ins = mm3(gate_ps[0:ROUTE_COLS, 0:GT], route_h[:, c, :], route_l[:, c, :], x2_h[:, c, :],
                              x2_l[:, c, :], c == 0, c == DH - 1)
                ins.then_inc(pe_route, 1)

            def turn_route(g):
                pe.wait_ge(act_route, g + 1)
                for t in range(TILES):
                    ins = pe.transpose(gate_ps[0:TT, t * ROUTE_COLS:(t + 1) * ROUTE_COLS],
                                       route_sb[:, t * TT:(t + 1) * TT], ident[0:ROUTE_COLS, 0:ROUTE_COLS])
                ins.then_inc(pe_turn_route, 1)

            def turn_fold(g):
                pe.wait_ge(pool_fold, DH * g + 2)
                for x in range(2):
                    for img in range(PAIR):
                        for m in range(DH):
                            c = img * DIM + m * P
                            ins = pe.transpose(turn[0:NFP, x, c:c + P], folded[:, m, x, img, :], ident[:, :])
                ins.then_inc(pe_turn_fold, 1)

            def dft(g):
                pe.wait_ge(dve_fold_lo, g + 1)
                for x in range(2):
                    ins = mm3(turn[0:NF, x, :], dft_h[:, x, 0:NF], dft_l[:, x, 0:NF], fold_h[:, x, :],
                              fold_l[:, x, :], True, True)
                ins.then_inc(pe_dft, 1)

            def inverse_dft(g):
                pe.wait_ge(dve_spec, 3 * g + 3)
                for m in range(DH):
                    for img in range(PAIR):
                        c = img * DIM + m * P
                        for x in range(2):
                            ins = pe.matmul(inverted[:, m, img, x, :], spec_y[:, x, c:c + P], inverse[:, x, :],
                                            start=True, stop=True)
                    ins.then_inc(pe_idft, 1)

            def turn_gated(g):
                pe.wait_ge(gate_done, g + 1)
                for t in range(TILES):
                    ins = pe.transpose(gate_ps[0:ROUTED, t * TT:(t + 1) * TT], gated[:, t, :], ident[0:TT, 0:TT])
                ins.then_inc(pe_turn_gated, 1)

            def base(m):
                for c in range(DH):
                    mm3(big[FFN_BANK[m]][:, 0:GT], base_h[:, c, m * P:(m + 1) * P],
                        base_l[:, c, m * P:(m + 1) * P], x2_h[:, c, :], x2_l[:, c, :], c == 0, False)

            def routed(g, m):
                pe.wait_ge(dve_gated_lo, g + 1)
                mm3(big[FFN_BANK[m]][:, 0:GT], routedb_h[:, m * P:(m + 1) * P],
                    routedb_l[:, m * P:(m + 1) * P], gated_h[:, :], gated_l[:, :], False, True).then_inc(pe_ffn, 1)

            def mixer_out(g, m):
                for c in range(DH):
                    if m == 0:
                        pe.wait_ge(dve_y_lo, DH * g + c + 1)
                    ins = mm3(big[OUT_BANK[m]][:, 0:GT], outw_h[:, c, m * P:(m + 1) * P],
                              outw_l[:, c, m * P:(m + 1) * P], y_h[:, c, :], y_l[:, c, :], c == 0, c == DH - 1)
                ins.then_inc(pe_out, 1)

            def first_half(i):
                mid, back, tail = i - 1, i - 2, i - 3
                if exists(mid):
                    if not exists(mid - 1):
                        pe.wait_ge(dve_weight_lo, len(DVE_SPLITS))
                    pe.wait_ge(dve_x1_lo, mid + 1)
                    for m in range(DH):
                        if not exists(mid - 1):
                            pe.wait_ge(act_h, DH + m + 1)
                        if m == 1 and exists(back):
                            pe.wait_ge(dve_mod, DH * back + 1)
                        for c in range(DH):
                            ins = mm3(big[IN_BANK[m]][:, 0:GT], inw_h[:, c, m * P:(m + 1) * P],
                                      inw_l[:, c, m * P:(m + 1) * P], x1_h[:, c, :], x1_l[:, c, :],
                                      c == 0, c == DH - 1)
                        ins.then_inc(pe_in, 1)
                if exists(tail):
                    route(tail)
                if exists(mid):
                    if exists(back):
                        pe.wait_ge(dve_mod, DH * back + 2)
                    mlp_up(mid, 0)
                if exists(tail):
                    turn_route(tail)
                if exists(back):
                    if not exists(back - 1):
                        pe.wait_ge(pool_weight_lo, len(POOL_SPLITS))
                        pe.wait_ge(spectrum_ready, 1)
                    turn_fold(back)
                if exists(mid):
                    for k in (1, 2):
                        pe.wait_ge(act_in, DH * mid + k)
                        mlp_up(mid, k)
                    for k in (3, 4):
                        pe.wait_ge(act_gelu, HC * mid + k - 2)
                        mlp_up(mid, k)
                if exists(back):
                    dft(back)
                if exists(mid):
                    pe.wait_ge(act_gelu, HC * mid + 3)
                    mlp_up(mid, 5)
                if exists(tail):
                    pe.wait_ge(act_gelu, HC * mid + 4)
                    base(0)
                    turn_gated(tail)
                    pe.wait_ge(act_gelu, HC * mid + 5)
                    base(1)
                if exists(mid):
                    pe.wait_ge(act_gelu, HC * mid + 6)
                for m in range(DH):
                    if exists(mid):
                        mlp_up(mid, 6, (m,))
                    if exists(tail):
                        routed(tail, m)
                if exists(mid):
                    if exists(tail):
                        pe.wait_ge(dve_result, DH * tail + 1)
                    mlp_up(mid, 7)

            def step(i, slot):
                front, mid, back, tail = i, i - 1, i - 2, i - 3
                first_half(i)
                first, second = isinstance(i, int) and i == 0, isinstance(i, int) and i == 1
                if first:
                    embed_first()
                    pe.wait_ge(ident_in, 16)
                elif not second:
                    if exists(tail):
                        pe.wait_ge(dve_result, DH * tail + 2)
                    else:
                        pe.wait_ge(act_gelu, HC * mid + 5)
                    embed(front, 0)
                if exists(back):
                    inverse_dft(back)
                if exists(mid):
                    pe.wait_ge(act_gelu, HC * mid + 7)
                    if not second:
                        embed(front, 1)
                if exists(back):
                    pe.wait_ge(act_gelu, HC * mid + 8)
                    mixer_out(back, 0)
                    pe.wait_ge(act_h, DH * front + 1)
                    mixer_out(back, 1)
                pe.wait_ge(act_h, DH * front + 2)
                to_tokens(turn, h_sb[:, slot], pe_turn_h)
                if exists(back):
                    pe.wait_ge(dve_h2, DH * back + 2)
                    to_tokens(turn2, h_sb[:, (slot + 1) % SLOTS], pe_turn_h2)
                if first:
                    embed(1, 0)
                if exists(mid):
                    if not exists(mid - 1):
                        pe.wait_ge(pool_weight_lo, POOL_SPLITS.index("w2") + 1)
                        pe.wait_ge(act_gelu, HC * mid + 8)
                    mlp_down(mid, 0, range(8))
                    mlp_down(mid, 1, range(4))
                pe.wait_ge(act_norm1, front + 1)
                pe.wait_ge(dve_norm1, front + 1)
                to_features(turn, norm1, pe_turn_x1)
                if first:
                    embed(1, 1)
                    setup_products()
                if exists(mid):
                    mlp_down(mid, 1, range(4, 8))
                if exists(back):
                    pe.wait_ge(act_norm2, back + 1)
                    pe.wait_ge(dve_norm2, back + 1)
                    to_features(turn2, norm2, pe_turn_x2)

            def drain():
                mid, back, tail = GROUPS - 1, GROUPS - 2, GROUPS - 3
                first_half(GROUPS)
                pe.wait_ge(act_gelu, HC * mid + 7)
                mlp_down(mid, 0, range(4))
                inverse_dft(back)
                mlp_down(mid, 0, range(4, 8))
                pe.wait_ge(act_gelu, HC * mid + 8)
                mixer_out(back, 0)
                pe.wait_ge(dve_result, DH * tail + 2)
                mixer_out(back, 1)
                pe.wait_ge(dve_h2, DH * back + 1)
                mlp_down(mid, 1, range(4))
                pe.wait_ge(dve_h2, DH * back + 2)
                to_tokens(turn2, h_sb[:, back % SLOTS], pe_turn_h2)
                mlp_down(mid, 1, range(4, 8))
                turn_fold(mid)
                pe.wait_ge(act_norm2, back + 1)
                pe.wait_ge(dve_norm2, back + 1)
                to_features(turn2, norm2, pe_turn_x2)
                back, tail = GROUPS - 1, GROUPS - 2
                dft(back)
                route(tail)
                turn_route(tail)
                inverse_dft(back)
                pe.wait_ge(dve_mod, DH * back + 2)
                for m in range(DH):
                    mixer_out(back, m)
                pe.wait_ge(dve_h2, DH * back + 2)
                to_tokens(turn2, h_sb[:, back % SLOTS], pe_turn_h2)
                turn_gated(tail)
                for m in range(DH):
                    base(m)
                pe.wait_ge(act_norm2, back + 1)
                pe.wait_ge(dve_norm2, back + 1)
                to_features(turn2, norm2, pe_turn_x2)
                pe.wait_ge(dve_gated_lo, tail + 1)
                route(back)
                turn_route(back)
                for m in range(DH):
                    routed(tail, m)
                for m in range(DH):
                    pe.wait_ge(dve_result, DH * tail + m + 1)
                    base(m)
                turn_gated(back)
                for m in range(DH):
                    routed(back, m)

            for i in range(3):
                step(i, i)
            with pe.Fori(3, LOOP_END, SLOTS) as i:
                for slot in range(SLOTS):
                    step(i + slot, slot)
            for i in range(GROUPS - 2, GROUPS):
                step(i, i % SLOTS)
            drain()


def shape_constants():
    f, t = np.arange(NF), np.arange(N_TOK)
    angle = 2 * np.pi * ((f[:, None] * t[None, :]) % N_TOK) / N_TOK
    cos, sin = np.cos(angle), np.sin(angle)
    sin[[0, HALF], :] = 0.0
    sin[:, [0, HALF]] = 0.0
    weight = np.where((f == 0) | (f == HALF), 1.0, 2.0) / N_TOK
    fwd = cos[:, :NF].copy()
    fwd[HALF] *= 0.5
    earlier = np.tril(np.ones((EXPERTS, EXPERTS)), -1) * -TINY
    c32 = lambda a: np.ascontiguousarray(a, dtype=np.float32)
    return {
        "ident": c32(np.eye(P)),
        "cos_fwd": c32(fwd),
        "sin_fwd": c32(-sin[:, :NF]),
        "cos_inv": c32(np.pad(cos[:, :NF], ((0, 0), (0, INV - NF)))),
        "sin_inv": c32(np.pad(-sin[:, :NF], ((0, 0), (0, INV - NF)))),
        "cos_tap": c32((weight[:, None] * cos[:, :TAPS]).T),
        "sin_tap": c32((weight[:, None] * -sin[:, :TAPS]).T),
        "rank_thr": c32(np.broadcast_to(earlier, (TT, TILES, EXPERTS, EXPERTS)).reshape(TT, -1)),
    }


def kernel(**inputs):
    import concourse.bacc as bacc
    from concourse.bass_utils import run_bass_kernel_spmd

    a = {k: np.asarray(v) for k, v in inputs.items()}
    x = a["x"].reshape(IMAGES, CHANNELS, GRID, PATCH, GRID, PATCH).transpose(0, 1, 3, 5, 2, 4)
    x = x.reshape(IMAGES, N_TOK, FLAT).reshape(GROUPS, GT, KT, P).transpose(0, 3, 2, 1)
    consts = shape_constants()
    pre = "L0_"
    columns = [a[pre + k].reshape(-1, P) for k in
               ("attn_in_b", "attn_mod_b2", "attn_out_b", "ffn_base_b", "attn_mod_b1")]
    route_column = np.zeros((1, P), np.float32)
    route_column[0, ROUTED:ROUTE_COLS] = a[pre + "ffn_router_b"]
    biases = np.concatenate([*columns, route_column]).T
    arrays = {
        "xg": x,
        "tok_w": a[pre + "tok_W"],
        "in_w": a[pre + "attn_in_w"],
        "w1": a[pre + "attn_mod_w1"],
        "w2": a[pre + "attn_mod_w2"],
        "taps_t": a[pre + "attn_kernel"].T,
        "out_w": a[pre + "attn_out_w"],
        "base_wt": a[pre + "ffn_base_W"].T,
        "shared_a": a[pre + "ffn_shared_A"],
        "shared_bt": a[pre + "ffn_shared_B"].T,
        "route_w": np.concatenate([a[pre + "ffn_routed_A"].reshape(ROUTED, DIM), a[pre + "ffn_router_W"]]).T,
        "routed_bt": a[pre + "ffn_routed_B"].transpose(0, 2, 1).reshape(ROUTED, DIM),
        "biases": biases,
        **consts,
    }
    arrays = {k: np.ascontiguousarray(v) for k, v in arrays.items()}
    nc = bacc.Bacc("TRN2", target_bir_lowering=False, num_devices=1)
    args = [nc.dram_tensor("dram_" + k, v.shape, mybir.dt.from_np(v.dtype), kind="ExternalInput").ap()
            for k, v in arrays.items()]
    out = nc.dram_tensor("out", (DIM, IMAGES * N_TOK), F32, kind="ExternalOutput").ap()
    tower_program(nc, *args, out)
    r = run_bass_kernel_spmd(nc, [{"dram_" + k: v for k, v in arrays.items()}], core_ids=[0])
    return np.ascontiguousarray(r.results[0]["out"].T).reshape(IMAGES, N_TOK, DIM)
```
